# Optimizing a Trainium2 kernel written in Bass

```python
import numpy as np
import jax
import jax.numpy as jnp

def _softmax(x, axis=-1):
    return jax.nn.softmax(x, axis=axis)

def _gelu(x):
    return jax.nn.gelu(x, approximate=True)

def _silu(x):
    return jax.nn.silu(x)

def _sigmoid(x):
    return jax.nn.sigmoid(x)

def _layernorm(x, axis=-1, eps=1e-05):
    m = jnp.mean(x, axis=axis, keepdims=True)
    v = jnp.var(x, axis=axis, keepdims=True)
    return (x - m) / jnp.sqrt(v + eps)

def _scatter_add(tgt, idx, src, axis=0):
    return tgt.at[idx].add(src)

def _segment_sum(src, seg, n):
    return jax.ops.segment_sum(src, seg, n)
kernel_name = 'mk_conv_preact_d2_conv_nhwc128_r2_40e1d7'

def setup_inputs(seed: int=0):
    np.random.seed(seed)
    _w = jnp.asarray

    def _rec_inputs():
        import jax
        import jax.numpy as jnp
        _gk = jax.random.key(seed)
        x = -7.109e-05 + 0.9999 * jax.random.normal(jax.random.fold_in(_gk, 1), (16, 64, 128, 64), jnp.float32)
        return x
    x = _rec_inputs()

    def _L0_conv_setup():
        import jax, jax.numpy as jnp
        import numpy as np
        GAMMA = 4

        def _rel_indices(n):
            idx = jnp.arange(n, dtype=jnp.float32)
            d = idx[None, :] - idx[:, None]
            return jnp.stack([d, d * d], axis=-1)
        key = jax.random.key(seed)
        k1, k2, k3, k4 = jax.random.split(key, 4)
        b, w, n, c = (16, 64, 128, 64)
        x = jax.random.normal(k1, (b, w, n, c), dtype=jnp.float32)
        att_std = 0.01
        attention_centers = att_std * jax.random.normal(k2, (GAMMA, 1), dtype=jnp.float32)
        attention_spreads = 1.0 + att_std * jax.random.normal(k3, (GAMMA, 1), dtype=jnp.float32)
        token_proj_n_bias = 0.01 * jax.random.normal(k4, (1, n, 1), dtype=jnp.float32)
        return {'x': x, 'attention_centers': attention_centers, 'attention_spreads': attention_spreads, 'token_proj_n_bias': token_proj_n_bias}
    _L0_conv_all = _L0_conv_setup()
    _L0_conv_in = {k: v for k, v in _L0_conv_all.items() if k in ('attention_centers', 'attention_spreads', 'token_proj_n_bias')}
    del _L0_conv_all

    def _L1_conv_setup():
        import jax, jax.numpy as jnp
        import numpy as np
        B, H, W_DIM, C = (8, 64, 128, 64)
        K = 9

        def conv1d_same(y, W):
            return jax.lax.conv_general_dilated(y, W, window_strides=(1,), padding='SAME', dimension_numbers=('NWC', 'WIO', 'NWC'))
        key = jax.random.key(seed)
        kx, kw = jax.random.split(key)
        x = jax.random.normal(kx, (B, H, W_DIM, C), dtype=jnp.float32)
        W = jax.random.normal(kw, (K, C, C), dtype=jnp.float32) * 0.02
        return {'x': x, 'W': W}
    _L1_conv_all = _L1_conv_setup()
    _L1_conv_in = {k: v for k, v in _L1_conv_all.items() if k in ('W',)}
    del _L1_conv_all
    return {'x': x, 'L0_conv_attention_centers': _L0_conv_in['attention_centers'], 'L0_conv_attention_spreads': _L0_conv_in['attention_spreads'], 'L0_conv_token_proj_n_bias': _L0_conv_in['token_proj_n_bias'], 'L1_conv_W': _L1_conv_in['W']}

def reference(x, L0_conv_attention_centers, L0_conv_attention_spreads, L0_conv_token_proj_n_bias, L1_conv_W):
    import jax
    import jax.numpy as jnp

    def _L0_conv_ref(x, attention_centers, attention_spreads, token_proj_n_bias):
        import jax, jax.numpy as jnp
        import numpy as np
        GAMMA = 4

        def _rel_indices(n):
            idx = jnp.arange(n, dtype=jnp.float32)
            d = idx[None, :] - idx[:, None]
            return jnp.stack([d, d * d], axis=-1)
        b, w, n, c = x.shape
        s = attention_centers.shape[0]
        v = c // s
        pos_proj = -0.5 * jnp.concatenate([-2.0 * attention_centers * attention_spreads, attention_spreads], axis=-1)
        rel = _rel_indices(n)
        pos_score = jnp.einsum('mnd,sd->mns', rel, pos_proj)
        posmap = jax.nn.softmax(pos_score, axis=1)
        xr = x.reshape(b, w, n, v, s)
        out = jnp.einsum('mns,bwnvs->bwmvs', posmap, xr)
        out = out + token_proj_n_bias[None, :, :, :, None]
        return out.reshape(b, w, n, c)

    def _L1_conv_ref(x, W):
        import jax, jax.numpy as jnp
        import numpy as np
        B, H, W_DIM, C = (8, 64, 128, 64)
        K = 9

        def conv1d_same(y, W):
            return jax.lax.conv_general_dilated(y, W, window_strides=(1,), padding='SAME', dimension_numbers=('NWC', 'WIO', 'NWC'))
        rows = jnp.moveaxis(x, 1, 0)
        row0 = rows[0]

        def step(carry, row):
            new = row + jax.nn.relu(conv1d_same(carry, W))
            return (new, new)
        _, outs = jax.lax.scan(step, row0, rows[1:])
        out = jnp.concatenate([row0[None], outs], axis=0)
        return jnp.moveaxis(out, 0, 1)

    def _gn(v, G=32, eps=1e-05):
        B_, H_, W_, C_ = v.shape
        g = v.reshape(B_, H_, W_, G, C_ // G)
        m = jnp.mean(g, axis=(1, 2, 4), keepdims=True)
        s = jnp.var(g, axis=(1, 2, 4), keepdims=True)
        return ((g - m) / jnp.sqrt(s + eps)).reshape(v.shape)

    def _ln_c(v, eps=1e-06):
        m = jnp.mean(v, axis=-1, keepdims=True)
        s = jnp.var(v, axis=-1, keepdims=True)
        return (v - m) / jnp.sqrt(s + eps)

    def _ln_t(v, eps=1e-05):
        m = jnp.mean(v, axis=-1, keepdims=True)
        s = jnp.var(v, axis=-1, keepdims=True)
        return (v - m) / jnp.sqrt(s + eps)

    def _to_tokens(v):
        B_, H_, W_, C_ = v.shape
        return v.reshape(B_, H_ * W_, C_)

    def _from_tokens(t, like):
        return t.reshape(like.shape)
    x = x + _L0_conv_ref(_gn(x), L0_conv_attention_centers, L0_conv_attention_spreads, L0_conv_token_proj_n_bias)
    x = x + _L1_conv_ref(_gn(x), L1_conv_W)
    return x

_drawn_inputs = setup_inputs


def setup_inputs(seed=0):
    import zlib

    import numpy as np

    out = dict(_drawn_inputs(seed))
    spreads = {}
    factors = {'L0_conv_attention_centers': 8.0,
     'L0_conv_attention_spreads': 8.0,
     'L0_conv_token_proj_n_bias': 7.959}
    for name, (base, spread) in spreads.items():
        noise = np.random.default_rng([zlib.crc32(name.encode()), seed]).standard_normal(out[name].shape)
        drawn = base * np.exp(spread * noise) if base else spread * noise
        out[name] = jnp.asarray(drawn.astype(out[name].dtype))
    for name, factor in factors.items():
        out[name] = (out[name] * factor).astype(out[name].dtype)
    return out
```

```python
import concourse.bass as bass
from concourse import mybir
from contextlib import ExitStack



def mix_and_scan_kernel(nc: bass.Bass, x: bass.AP, centers: bass.AP, spreads: bass.AP,
                        token_bias: bass.AP, conv_w: bass.AP, out: bass.AP):
    f32 = mybir.dt.float32
    f32r = mybir.dt.float32r
    i32 = mybir.dt.int32
    ALU = mybir.AluOpType
    ACT = mybir.ActivationFunctionType
    AX = mybir.AxisListType

    B, H, N, C = x.shape
    S = centers.shape[0]
    V = C // S
    K = conv_w.shape[0]
    PAD = (K - 1) // 2
    P = 128
    J = N // 2
    G = 32
    CG = C // G
    EPS = 1e-5
    D = PAD + 1
    EDGE = PAD // 2
    W = B // 2
    NS = 2
    WS = W // NS
    SW = WS * J
    STEPS = 8
    ITERS = H // STEPS
    CH = 4
    CR = H // CH
    CC = CR * C
    HR = CR // 2
    RG = 4
    TURN_STEP = {4: 0, 5: 1, 7: 2}
    HALF_COUNT = H // 2 * CG

    x_nat = x.rearrange("b h (j q) c -> b q j h c", q=2)
    out_pairs = out.rearrange("b h (j q) c -> b h j (q c)", q=2)

    with ExitStack() as ctx:
        def sb(name, shape, dt=f32):
            return ctx.enter_context(nc.sbuf_tensor(name, shape, dt))

        def pb(name):
            return ctx.enter_context(nc.psum_tensor(name, [P, 512], f32))

        def sem(name):
            return ctx.enter_context(nc.semaphore(name))

        x1_paired = sb("x1_paired", [P, H * W * J])
        rows = sb("rows", [P, 2, RG, W, J])
        x_sb = sb("x_sb", [P, H * C])
        x_swap = sb("x_swap", [P, 2, HR, 2, C])
        xs = sb("xs", [P, CC])
        xh = sb("xh", [P, CC], f32r)
        xl = sb("xl", [P, CC], f32r)
        wh = sb("wh", [P, D, P], f32r)
        wl = sb("wl", [P, D, P], f32r)
        mix_h = sb("mix_h", [P, S, P], f32r)
        mix_l = sb("mix_l", [P, S, P], f32r)
        JP = J + 2 * EDGE
        carry_h = [sb(f"carry_h{s}", [P, WS, JP], f32r) for s in range(NS)]
        carry_l = [sb(f"carry_l{s}", [P, WS, JP], f32r) for s in range(NS)]
        carry = [sb(f"carry{s}", [P, SW]) for s in range(NS)]
        total = [sb(f"total{s}", [P, SW]) for s in range(NS)]
        staged = sb("staged", [P, 2, NS * SW])
        ident = sb("ident", [P, P])
        st1 = sb("st1", [P, 2, G, 3])
        dev = sb("dev", [P, 2, G])
        dev2 = sb("dev2", [P, 2, G])
        m2 = sb("m2", [P, 2, G])
        var1 = sb("var1", [P, G])
        rstd1 = sb("rstd1", [P, G])
        rstd1_c = sb("rstd1_c", [P, 2, G, CG])
        mean_rstd = sb("mean_rstd", [P, 2, G, CG])
        shift1 = sb("shift1", [P, 2])
        st2 = sb("st2", [P, 2 * CH, 6])
        mv = sb("mv", [P, 2])
        dev_c = sb("dev_c", [P, 1])
        var_p = sb("var_p", [P, 1])
        var2 = sb("var2", [P, 1])
        rstd2 = sb("rstd2", [P, B])
        shift2 = sb("shift2", [P, B])
        bias_col = sb("bias_col", [P, 1])
        half_power = sb("half_power", [P, G])
        inv256 = sb("inv256", [P, P])
        minus_avg = sb("minus_avg", [P, 1])
        group_avg = sb("group_avg", [P, 2, G, CG])
        w_raw = x1_paired[:, 0:D * P].rearrange("p (d m) -> p d m", d=D)
        at = D * P

        def scratch(n):
            nonlocal at
            at += n
            return x1_paired[:, at - n:at]
        dist = scratch(P)
        dist_i = scratch(P).bitcast(i32)
        dist2 = scratch(P)
        score = scratch(S * P).rearrange("p (s n) -> p s n", s=S)
        lin = scratch(S * P).rearrange("p (s n) -> p s n", s=S)
        prob = scratch(S * P).rearrange("p (s n) -> p s n", s=S)
        posmap = scratch(S * P).rearrange("p (s n) -> p s n", s=S)
        att_row = scratch(2 * S)
        proj_row = scratch(2 * S)
        proj = scratch(2 * S)
        neg_max = scratch(S)
        peak = scratch(S)
        exp_sum = scratch(S)
        inv_sum = scratch(S)
        ones_row = scratch(P)
        group_of = scratch(G)

        ps_conv = [pb(f"ps_conv{s}") for s in range(NS)]
        ps_mix = [pb(f"ps_mix{n}") for n in range(2)]
        ps_in = [pb(f"ps_in{n}") for n in range(2)]
        ps_out = pb("ps_out")
        ps_small = pb("ps_small")
        mean1 = ps_small[:, 0:G]
        var1_ps = ps_small[:, G:2 * G]
        shift1_ps = ps_small[:, 64:65]
        mean2 = ps_small[:, 66:67]
        var2_ps = ps_small[:, 68:69]

        w_loaded = sem("w_loaded")
        small_loaded = sem("small_loaded")
        w_zeroed = sem("w_zeroed")
        w_high = sem("w_high")
        setup_dve = sem("setup_dve")
        consts = sem("consts")
        pool_chain = sem("pool_chain")
        pool_consts = sem("pool_consts")
        proj_ps = sem("proj_ps")
        score_ready = sem("score_ready")
        prob_ready = sem("prob_ready")
        posmap_ready = sem("posmap_ready")
        posmap_t = sem("posmap_t")
        mix_high = sem("mix_high")
        setup_done = sem("setup_done")
        x_loaded = [sem(f"x_loaded{c}") for c in range(CH)]
        swapped = [sem(f"swapped{c}") for c in range(CH)]
        stats1_done = sem("stats1_done")
        mean1_ps = sem("mean1_ps")
        dev_ready = sem("dev_ready")
        dev2_ready = sem("dev2_ready")
        m2_ready = sem("m2_ready")
        var1_in_ps = sem("var1_in_ps")
        var1_ready = sem("var1_ready")
        rstd1_ready = sem("rstd1_ready")
        rstd1_c_ready = sem("rstd1_c_ready")
        mean_rstd_ready = sem("mean_rstd_ready")
        shift1_in_ps = sem("shift1_in_ps")
        shift1_ready = sem("shift1_ready")
        xs_ready = sem("xs_ready")
        xh_ready = sem("xh_ready")
        xl_ready = sem("xl_ready")
        mix_done = [sem(f"mix_done{n}") for n in range(2)]
        x1_done = [sem(f"x1_done{n}") for n in range(2)]
        in_turned = sem("in_turned")
        in_kept = sem("in_kept")
        stats2_done = sem("stats2_done")
        mv_ready = sem("mv_ready")
        mean2_ps = sem("mean2_ps")
        dev_c_ready = sem("dev_c_ready")
        var_p_ready = sem("var_p_ready")
        var2_in_ps = sem("var2_in_ps")
        var2_ready = sem("var2_ready")
        rstd2_ready = sem("rstd2_ready")
        shift2_ready = sem("shift2_ready")
        rows_ready = sem("rows_ready")
        conv_done = [sem(f"conv_done{s}") for s in range(NS)]
        carry_ready = [sem(f"carry_ready{s}") for s in range(NS)]
        high_ready = [sem(f"high_ready{s}") for s in range(NS)]
        low_ready = [sem(f"low_ready{s}") for s in range(NS)]
        total_ready = [sem(f"total_ready{s}") for s in range(NS)]
        out_turned = sem("out_turned")
        out_staged = sem("out_staged")
        stored = [sem(f"stored{n}") for n in range(2)]

        def x1_chunk_half(wave, b, c, u):
            if wave == 1:
                v = x1_paired[:, bass.ds(b * (H * J) + c * CR * J, CR * J)]
                v = v.rearrange("p (r h j) -> p h r j", r=2, j=J)
                return v[:, RG * u:RG * u + RG, :, :]
            v = x1_paired[:, :].rearrange("p (h w j) -> p h w j", w=W, j=J)
            v = v[:, c * CR:(c + 1) * CR, bass.ds(b, 1), :]
            v = v.rearrange("p (r h) w j -> p h r (w j)", r=2)
            return v[:, RG * u:RG * u + RG, :, :]

        def x1_rows(wave, it, row, n, b0, nb):
            if wave == 0:
                v = x1_paired[:, bass.ds(it * (STEPS * W * J) + row * W * J, n * W * J)]
                return v.rearrange("p (h w j) -> p h w j", h=n, w=W)[:, :, b0:b0 + nb, :]
            v = x1_paired[:, :].rearrange("p (w h j) -> p h w j", w=W, j=J)
            return v[:, bass.ds(it * STEPS + row, n), b0:b0 + nb, :]

        def alone(eng, done):
            eng.wait_ge(done, 1)

        def held(eng, n):
            return n if isinstance(n, int) else eng.to_reg(n)

        def is_zero(n):
            return isinstance(n, int) and n == 0

        def is_last(it):
            return isinstance(it, int) and it == ITERS - 1

        block = ctx.enter_context(nc.Block())

        @block.sync
        def _(sp):
            def load_chunk(b, c):
                for q in range(2):
                    src = x_nat[bass.ds(b, 1), q, :, c * CR:(c + 1) * CR, :]
                    sp.dma_start(x_sb[q * J:(q + 1) * J, c * CC:(c + 1) * CC].rearrange("j (h c) -> j h c", c=C),
                                 src.rearrange("b j h c -> (b j) h c")).then_inc(x_loaded[c], 16)

            def swap_chunk(b, c):
                n = b * CH + c
                mixed, turned = held(sp, n + 1), held(sp, 2 * (n - 1))
                alone(sp, w_zeroed)
                for m in range(2):
                    sp.wait_ge(x1_done[m], mixed)
                if not (isinstance(b, int) and n < 2):
                    sp.wait_ge(in_turned, turned)
                for q in range(2):
                    for r in range(2):
                        src = x_sb[q * J:(q + 1) * J, c * CC + r * HR * C:c * CC + (r + 1) * HR * C]
                        sp.dma_start(x_swap[r * J:(r + 1) * J, c % 2, :, q, :],
                                     src.rearrange("j (h c) -> j h c", c=C)).then_inc(swapped[c], 16)

            def batch(b, more):
                for c in range(CH):
                    swap_chunk(b, c)
                    if more:
                        copied = held(sp, (b + 1) * 64)
                        alone(sp, w_zeroed)
                        sp.wait_ge(swapped[c], copied)
                        load_chunk(b + 1, c)

            for c in range(CH):
                load_chunk(0, c)
            sp.wait_ge(w_zeroed, 1)
            for q in range(2):
                for o in range(2):
                    ds = [d for d in range(D) if 0 <= 2 * d + q - o < K]
                    k0 = 2 * ds[0] + q - o
                    sp.dma_start(w_raw[q * C:(q + 1) * C, ds[0]:ds[-1] + 1, o * C:(o + 1) * C],
                                 conv_w[k0:k0 + 2 * len(ds) - 1:2, :, :].rearrange("k c o -> c k o")
                                 ).then_inc(w_loaded, 16)
            batch(0, True)
            with sp.Fori(1, W) as b:
                batch(b, True)
            batch(W, True)
            with sp.Fori(W + 1, B - 1) as b:
                batch(b, True)
            batch(B - 1, False)

        @block.gpsimd
        def _(pool):
            nc.gpsimd.memset(ident[:, :], 0.0).then_inc(pool_chain, 1)
            nc.gpsimd.memset(group_of, 0.0).then_inc(pool_chain, 1)
            pool.wait_ge(pool_chain, 2)
            nc.gpsimd.affine_select(out=ident[:, :], in_=ident[:, :], compare_op=ALU.not_equal, fill=1.0,
                                    base=0, pattern=[[-1, P]], channel_multiplier=1).then_inc(pool_consts, 1)
            n = 2
            for q in range(2):
                for e in range(CG):
                    nc.gpsimd.affine_select(out=group_of, in_=group_of, compare_op=ALU.not_equal,
                                            fill=1.0 / (2 * CG), base=-(q * C + e), pattern=[[-CG, G]],
                                            channel_multiplier=1).then_inc(pool_chain, 1)
                    n += 1
                    pool.wait_ge(pool_chain, n)
            for q in range(2):
                for e in range(CG):
                    nc.gpsimd.tensor_copy(group_avg[:, q, :, e], group_of).then_inc(pool_consts, 1)
            nc.gpsimd.iota(dist_i, pattern=[[1, 2], [2, J]], base=0,
                           channel_multiplier=-1).then_inc(pool_consts, 1)

            def rstd1_of(b):
                pool.wait_ge(var1_ready, b + 1)
                if not is_zero(b):
                    pool.wait_ge(mean_rstd_ready, b)
                nc.gpsimd.tensor_tensor(rstd1[:, :], var1[:, :], half_power[:, :], ALU.pow).then_inc(rstd1_ready, 1)
                alone(pool, consts)
                pool.wait_ge(rstd1_ready, b + 1)
                for q in range(2):
                    nc.gpsimd.tensor_copy(rstd1_c[:, q, :, :],
                                          rstd1[:, :].unsqueeze(2).to_broadcast([P, G, CG])
                                          ).then_inc(rstd1_c_ready, 1)
                pool.wait_ge(rstd1_c_ready, 2 * b + 2)

            def scale_chunk(b, c):
                src = x_sb[:, c * CC:(c + 1) * CC].rearrange("p (h c) -> p h c", c=C)
                r = rstd1_c[:, 0, :, :].rearrange("p g e -> p (g e)").unsqueeze(1).to_broadcast([P, CR, C])
                nc.gpsimd.tensor_tensor(xs[:, :].rearrange("p (h c) -> p h c", c=C), src, r,
                                        ALU.mult).then_inc(xs_ready, 1)

            def low_chunk(b, c):
                n = b * CH + c
                pool.wait_ge(xh_ready, n + 1)
                if not is_zero(n):
                    for m in range(2):
                        pool.wait_ge(mix_done[m], n)
                nc.gpsimd.tensor_tensor(xl[:, :], xs[:, :], xh[:, :].bitcast(f32), ALU.subtract).then_inc(xl_ready, 1)
                pool.wait_ge(xl_ready, n + 1)

            def rstd2_of(b):
                pool.wait_ge(var2_ready, b + 1)
                nc.gpsimd.tensor_tensor(rstd2[:, bass.ds(b, 1)], var2[:, :], half_power[:, 0:1],
                                        ALU.pow).then_inc(rstd2_ready, 1)

            def prep(b, i, prev):
                if i == 0:
                    rstd1_of(b)
                if 1 <= i <= CH:
                    low_chunk(b, i - 1)
                if i < CH:
                    scale_chunk(b, i)
                if i == 3 and prev:
                    rstd2_of(b - 1)

            def add_carry(wave, it, i, s):
                t = (it + wave * ITERS) * STEPS + i
                pool.wait_ge(carry_ready[s], t + 1)
                if not is_zero(t):
                    pool.wait_ge(out_turned, t)
                nc.gpsimd.tensor_tensor(total[s][:, :].rearrange("p (w j) -> p w j", w=WS),
                                        x1_rows(wave, it, i, 1, s * WS, WS)[:, 0, :, :],
                                        carry[s][:, :].rearrange("p (w j) -> p w j", w=WS),
                                        ALU.add).then_inc(total_ready[s], 1)

            def iteration(wave, it, b, prev):
                for i in range(STEPS):
                    for s in range(NS):
                        add_carry(wave, it, i, s)
                    if b is not None:
                        prep(b, i, prev)

            pool.wait_ge(consts, 1)
            for i in range(STEPS):
                prep(0, i, False)
            with pool.Fori(1, W) as b:
                for i in range(STEPS):
                    prep(b, i, True)
            rstd2_of(W - 1)
            iteration(0, 0, W, False)
            with pool.Fori(1, ITERS - 1) as it:
                iteration(0, it, it + W, True)
            iteration(0, ITERS - 1, B - 1, True)
            rstd2_of(B - 1)
            with pool.Fori(0, ITERS) as it:
                iteration(1, it, None, False)

        @block.scalar
        def _(act):
            act.dma_start(att_row[0:1, 0:S], centers.rearrange("s a -> a s")).then_inc(small_loaded, 16)
            act.dma_start(att_row[0:1, S:2 * S], spreads.rearrange("s a -> a s")).then_inc(small_loaded, 16)
            for q in range(2):
                act.dma_start(bias_col[q * J:(q + 1) * J, :],
                              token_bias.rearrange("a (j q) e -> q j (a e)", q=2)[q, :, :],
                              allow_slow_non_contiguous=True).then_inc(small_loaded, 16)
            for s in range(S):
                act.wait_ge(score_ready, s + 1)
                nc.scalar.activation(prob[:, s, :], score[:, s, :], ACT.Exp, bias=neg_max[:, s:s + 1],
                                     accum_out=exp_sum[:, s:s + 1]).then_inc(prob_ready, 1)

            def high_chunk(b, c):
                n = b * CH + c
                act.wait_ge(xs_ready, n + 1)
                if not is_zero(n):
                    for m in range(2):
                        act.wait_ge(mix_done[m], n)
                nc.scalar.activation(xh[:, :], xs[:, :], ACT.Copy).then_inc(xh_ready, 1)

            def keep_in(b, wave, bw, c, free):
                n = b * CH + c
                act.wait_ge(shift1_ready, b + 1)
                if free is not None:
                    for s in range(NS):
                        act.wait_ge(total_ready[s], free)
                for u in range(2):
                    half = held(act, 2 * n + u + 1)
                    alone(act, setup_done)
                    act.wait_ge(in_turned, half)
                    nc.scalar.activation(x1_chunk_half(wave, bw, c, u),
                                         ps_in[u][:, :].rearrange("p (h r j) -> p h r j", h=RG, r=2),
                                         ACT.Identity, bias=shift1[:, 0:1]).then_inc(in_kept, 1)

            def prep(b, wave, bw, i, prev, it):
                def over(steps):
                    return None if it is None else it * STEPS + steps
                if i == 0 and prev:
                    keep_in(b - 1, wave, bw - 1, 3, over(0))
                if 1 <= i <= CH:
                    high_chunk(b, i - 1)
                if i in TURN_STEP:
                    c = TURN_STEP[i]
                    keep_in(b, wave, bw, c, over(2 * (c + 1)))

            def norm_rows(wave, it, g, w):
                t = (it + wave * ITERS) * STEPS + g * RG
                if not (isinstance(t, int) and t < 2 * RG):
                    used = held(act, t - RG)
                    alone(act, setup_done)
                    for s in range(NS):
                        act.wait_ge(carry_ready[s], used)
                b = wave * W + w
                nc.scalar.activation(rows[:, g, :, w, :], x1_rows(wave, it, g * RG, RG, w, 1)[:, :, 0, :],
                                     ACT.Identity, scale=rstd2[:, b:b + 1],
                                     bias=shift2[:, b:b + 1]).then_inc(rows_ready, 1)

            def stage_out(t, buf):
                act.wait_ge(out_turned, t)
                if not (isinstance(t, int) and t <= 2):
                    act.wait_ge(stored[buf], (t - 1 - buf) * 16)
                nc.scalar.activation(staged[:, buf, :], ps_out[:, :], ACT.Copy).then_inc(out_staged, 1)

            def store_row(wave, h, t, buf):
                act.wait_ge(out_staged, t)
                src = staged[:, buf, :].rearrange("p (m f) -> p m f", f=P)
                for e in range(2):
                    dst = out_pairs[wave * W + e:(wave + 1) * W:2, bass.ds(h, 1), :, :]
                    act.dma_start(dst.rearrange("m h j f -> (h j) m f"),
                                  src[e * J:(e + 1) * J, :, :]).then_inc(stored[buf], 16)

            def iteration(wave, it, b, prev):
                first, last = is_zero(it), is_last(it)
                for i in range(STEPS):
                    t = (it + wave * ITERS) * STEPS + i
                    begins = first and i == 0
                    for s in range(NS):
                        if not (last and i == STEPS - 1):
                            act.wait_ge(carry_ready[s], t + 1)
                            nc.scalar.activation(carry_h[s][:, :, EDGE:EDGE + J],
                                                 carry[s][:, :].rearrange("p (w j) -> p w j", w=WS),
                                                 ACT.Copy).then_inc(high_ready[s], 1)
                        if s == 0 and not begins:
                            stage_out(t, (i + 1) % 2)
                        if s == 1 and not begins:
                            store_row(wave, it * STEPS + i - 1, t, (i + 1) % 2)
                        if not (last and i >= RG):
                            norm_rows(wave, it + i // RG, 1 - i // RG, (i % RG) * NS + s)
                    if b is not None:
                        prep(b, 1, it, i, prev, it)

            act.wait_ge(setup_done, 1)
            for i in range(STEPS):
                prep(0, 0, 0, i, False, None)
            with act.Fori(1, W) as b:
                for i in range(STEPS):
                    prep(b, 0, b, i, True, None)
            keep_in(W - 1, 0, W - 1, 3, None)
            act.wait_ge(shift2_ready, W)
            for w in range(W):
                norm_rows(0, 0, 0, w)
            iteration(0, 0, W, False)
            with act.Fori(1, ITERS - 1) as it:
                iteration(0, it, it + W, True)
            iteration(0, ITERS - 1, B - 1, True)
            keep_in(B - 1, 1, W - 1, 3, H)
            stage_out(H, 1)
            store_row(0, H - 1, H, 1)
            act.wait_ge(shift2_ready, B)
            for w in range(W):
                norm_rows(1, 0, 0, w)
            iteration(1, 0, None, False)
            with act.Fori(1, ITERS - 1) as it:
                iteration(1, it, None, False)
            iteration(1, ITERS - 1, None, False)
            stage_out(2 * H, 1)
            store_row(1, H - 1, 2 * H, 1)
            for n in range(2):
                act.wait_ge(stored[n], 2 * H // 2 * 32)

        @block.vector
        def _(dve):
            nc.vector.memset(w_raw, 0.0).then_inc(w_zeroed, 1)
            nc.vector.memset(half_power[:, :], -0.5).then_inc(consts, 1)
            nc.vector.memset(ones_row, 1.0)
            nc.vector.memset(inv256[:, :], 1.0 / (2 * P))
            nc.vector.memset(minus_avg[:, :], -1.0 / P)
            for s in range(NS):
                nc.vector.memset(carry_h[s][:, :, :].bitcast(f32), 0.0).then_inc(high_ready[s], 1)
                nc.vector.memset(carry_l[s][:, :, :].bitcast(f32), 0.0).then_inc(low_ready[s], 1)

            def stats1(b, half, first, count):
                for c in (2 * half, 2 * half + 1):
                    dve.wait_ge(x_loaded[c], 32 * (b + 1))
                v = x_sb[:, 2 * half * CC:2 * (half + 1) * CC]
                v = v.rearrange("p (h m g e) -> p m h e g", m=G // 2, g=2, e=CG)
                for m in range(first, first + count):
                    ins = nc.vector.bn_stats(st1[:, half, 2 * m:2 * m + 2, :].rearrange("p g k -> p (g k)"),
                                             v[:, m, :, :, :])
                if half == 1 and first + count == G // 2:
                    ins.then_inc(stats1_done, 1)

            for half in range(2):
                stats1(0, half, 0, G // 2)

            dve.wait_ge(small_loaded, 64)
            dve.wait_ge(pool_consts, 2 + 2 * CG)
            nc.vector.tensor_tensor(proj_row[0:1, 0:S], att_row[0:1, 0:S], att_row[0:1, S:2 * S], ALU.mult)
            nc.vector.tensor_scalar(proj_row[0:1, S:2 * S], att_row[0:1, S:2 * S], -0.5, None,
                                    ALU.mult).then_inc(setup_dve, 1)
            nc.vector.tensor_copy(dist, dist_i).then_inc(setup_dve, 1)
            dve.wait_ge(setup_dve, 2)
            nc.vector.tensor_tensor(dist2, dist, dist, ALU.mult).then_inc(setup_dve, 1)
            dve.wait_ge(proj_ps, 1)
            nc.vector.tensor_copy(proj, ps_small[:, 0:2 * S]).then_inc(setup_dve, 1)
            dve.wait_ge(setup_dve, 4)
            for s in range(S):
                nc.vector.tensor_scalar(lin[:, s, :], dist, proj[:, s:s + 1], None, ALU.mult).then_inc(setup_dve, 1)
            dve.wait_ge(setup_dve, 4 + S)
            for s in range(S):
                nc.vector.scalar_tensor_tensor(score[:, s, :], dist2, proj[:, S + s:S + s + 1], lin[:, s, :],
                                               ALU.mult, ALU.add).then_inc(setup_dve, 1)
            dve.wait_ge(setup_dve, 4 + 2 * S)
            nc.vector.reduce_max(peak, score, AX.X).then_inc(setup_dve, 1)
            dve.wait_ge(setup_dve, 5 + 2 * S)
            nc.vector.tensor_scalar(neg_max, peak, -1.0, None, ALU.mult).then_inc(score_ready, S)
            dve.wait_ge(prob_ready, S)
            nc.vector.reciprocal(inv_sum, exp_sum).then_inc(setup_dve, 1)
            dve.wait_ge(setup_dve, 6 + 2 * S)
            for s in range(S):
                nc.vector.tensor_scalar(posmap[:, s, :], prob[:, s, :], inv_sum[:, s:s + 1], None,
                                        ALU.mult).then_inc(posmap_ready, 1)
            dve.wait_ge(w_loaded, 64)
            nc.vector.tensor_copy(wh[:, :, :], w_raw).then_inc(w_high, 1)
            dve.wait_ge(w_high, 1)
            nc.vector.tensor_tensor(wl[:, :, :], w_raw, wh[:, :, :].bitcast(f32), ALU.subtract)
            dve.wait_ge(posmap_t, 1)
            turned = ps_in[0][:, :].rearrange("p (s j q) -> p s q j", s=S, q=2)
            for s in range(S):
                nc.vector.tensor_copy(mix_h[:, s, :].rearrange("p (q j) -> p q j", q=2), turned[:, s, :, :]
                                      ).then_inc(mix_high, 1)
            dve.wait_ge(mix_high, S)
            for s in range(S):
                ins = nc.vector.tensor_tensor(mix_l[:, s, :].rearrange("p (q j) -> p q j", q=2), turned[:, s, :, :],
                                              mix_h[:, s, :].bitcast(f32).rearrange("p (q j) -> p q j", q=2),
                                              ALU.subtract)
            ins.then_inc(setup_done, 1)

            def spread(row):
                return row.unsqueeze(1).unsqueeze(3).to_broadcast([P, 2, G, CG])

            def deviations1(b):
                dve.wait_ge(mean1_ps, b + 1)
                nc.vector.tensor_tensor(dev[:, :, :], st1[:, :, :, 1],
                                        mean1.unsqueeze(1).to_broadcast([P, 2, G]),
                                        ALU.subtract).then_inc(dev_ready, 1)
                dve.wait_ge(dev_ready, b + 1)
                nc.vector.tensor_tensor(dev2[:, :, :], dev[:, :, :], dev[:, :, :], ALU.mult).then_inc(dev2_ready, 1)
                dve.wait_ge(dev2_ready, b + 1)
                nc.vector.scalar_tensor_tensor(m2[:, :, :], dev2[:, :, :], float(HALF_COUNT), st1[:, :, :, 2],
                                               ALU.mult, ALU.add).then_inc(m2_ready, 1)

            def variance1(b):
                dve.wait_ge(var1_in_ps, b + 1)
                nc.vector.tensor_scalar(var1[:, :], var1_ps, 1.0 / HALF_COUNT, EPS, ALU.mult,
                                        ALU.add).then_inc(var1_ready, 1)

            def mean_rstd1(b):
                dve.wait_ge(rstd1_c_ready, 2 * b + 2)
                nc.vector.tensor_tensor(mean_rstd[:, :, :, :], spread(mean1), rstd1_c[:, :, :, :],
                                        ALU.mult).then_inc(mean_rstd_ready, 1)

            def keep_shift1(b):
                dve.wait_ge(shift1_in_ps, b + 1)
                if not is_zero(b):
                    dve.wait_ge(in_kept, 2 * CH * b)
                nc.vector.tensor_copy(shift1[:, 0:1], shift1_ps).then_inc(shift1_ready, 1)

            def mix_to_x1(b, c, m):
                dve.wait_ge(mix_done[m], b * CH + c + 1)
                for s in (2 * m, 2 * m + 1):
                    v = x_sb[:, c * CC + s:(c + 1) * CC:S]
                    ins = nc.vector.scalar_tensor_tensor(v, ps_mix[m][:, (s % 2) * CR * V:(s % 2 + 1) * CR * V],
                                                         bias_col[:, 0:1], v, ALU.add, ALU.add)
                ins.then_inc(x1_done[m], 1)

            def stats2(b, wave, bw, c, u):
                dve.wait_ge(in_kept, 2 * (b * CH + c) + u + 1)
                nc.vector.bn_stats(st2[:, 2 * c + u, :], x1_chunk_half(wave, bw, c, u)).then_inc(stats2_done, 1)

            def moments2(b):
                alone(dve, consts)
                dve.wait_ge(stats2_done, 2 * CH * (b + 1))
                nc.vector.bn_aggr(mv[:, :], st2[:, :, :].rearrange("p n k -> p (n k)")).then_inc(mv_ready, 1)

            def deviations2(b):
                dve.wait_ge(mean2_ps, b + 1)
                nc.vector.tensor_tensor(dev_c[:, :], mv[:, 0:1], mean2, ALU.subtract).then_inc(dev_c_ready, 1)
                dve.wait_ge(dev_c_ready, b + 1)
                nc.vector.scalar_tensor_tensor(var_p[:, :], dev_c[:, :], dev_c[:, 0:1], mv[:, 1:2],
                                               ALU.mult, ALU.add).then_inc(var_p_ready, 1)

            def variance2(b):
                dve.wait_ge(var2_in_ps, b + 1)
                nc.vector.tensor_scalar(var2[:, :], var2_ps, EPS, None, ALU.add).then_inc(var2_ready, 1)

            def shift2_of(b):
                dve.wait_ge(rstd2_ready, b + 1)
                nc.vector.scalar_tensor_tensor(shift2[:, bass.ds(b, 1)], mean2, -1.0, rstd2[:, bass.ds(b, 1)],
                                               ALU.mult, ALU.mult).then_inc(shift2_ready, 1)

            def prep(b, wave, bw, i, gap, prev, more):
                if i == 0 and gap == 1:
                    deviations1(b)
                if i == 0 and gap >= 2 and prev:
                    stats2(b - 1, wave, bw - 1, 2, gap - 2)
                if i == 0 and gap == 3:
                    variance1(b)
                if i == 1 and gap == 1:
                    mean_rstd1(b)
                if i == 1 and gap >= 2 and prev:
                    stats2(b - 1, wave, bw - 1, 3, gap - 2)
                if i == 1 and gap == 3:
                    keep_shift1(b)
                    if prev:
                        moments2(b - 1)
                if i == 2 and prev:
                    if gap == 1:
                        deviations2(b - 1)
                    if gap == 3:
                        variance2(b - 1)
                if 3 <= i < 3 + CH and gap in (0, 2):
                    mix_to_x1(b, i - 3, gap // 2)
                if i == 3 and gap == 3 and prev:
                    shift2_of(b - 1)
                if i in (6, 7) and gap in (1, 3):
                    stats2(b, wave, bw, i - 6, gap // 2)
                if i in (6, 7) and more:
                    stats1(b + 1, i - 6, G // 8 * gap, G // 8)

            def finish(b, wave, bw):
                for c in (2, 3):
                    for u in range(2):
                        stats2(b, wave, bw, c, u)
                moments2(b)
                deviations2(b)
                variance2(b)
                shift2_of(b)

            def iteration(wave, it, b, prev, more):
                last = is_last(it)
                for i in range(STEPS):
                    t = (it + wave * ITERS) * STEPS + i
                    for s in range(NS):
                        dve.wait_ge(conv_done[s], t + 1)
                        if i % RG == 0:
                            dve.wait_ge(rows_ready, 2 * t + W)
                        if not is_zero(t):
                            dve.wait_ge(total_ready[s], t)
                        nc.vector.scalar_tensor_tensor(
                            carry[s][:, :], ps_conv[s][:, 0:SW], 0.0,
                            rows[:, i // RG, i % RG, s * WS:(s + 1) * WS, :].rearrange("p w j -> p (w j)"),
                            ALU.max, ALU.add).then_inc(carry_ready[s], 1)
                        if b is not None:
                            prep(b, 1, it, i, 2 * s, prev, more)
                        if not (last and i == STEPS - 1):
                            dve.wait_ge(high_ready[s], t + 2)
                            nc.vector.tensor_tensor(carry_l[s][:, :, EDGE:EDGE + J],
                                                    carry[s][:, :].rearrange("p (w j) -> p w j", w=WS),
                                                    carry_h[s][:, :, EDGE:EDGE + J].bitcast(f32),
                                                    ALU.subtract).then_inc(low_ready[s], 1)
                        if b is not None:
                            prep(b, 1, it, i, 2 * s + 1, prev, more)

            for i in range(STEPS):
                for gap in range(4):
                    prep(0, 0, 0, i, gap, False, True)
            with dve.Fori(1, W) as b:
                for i in range(STEPS):
                    for gap in range(4):
                        prep(b, 0, b, i, gap, True, True)
            finish(W - 1, 0, W - 1)
            iteration(0, 0, W, False, True)
            with dve.Fori(1, ITERS - 1) as it:
                iteration(0, it, it + W, True, True)
            iteration(0, ITERS - 1, B - 1, True, False)
            for s in range(NS):
                nc.vector.memset(carry_h[s][:, :, :].bitcast(f32), 0.0).then_inc(high_ready[s], 1)
                nc.vector.memset(carry_l[s][:, :, :].bitcast(f32), 0.0).then_inc(low_ready[s], 1)
            finish(B - 1, 1, W - 1)
            with dve.Fori(0, ITERS - 1) as it:
                iteration(1, it, None, False, False)
            iteration(1, ITERS - 1, None, False, False)

        @block.tensor
        def _(pe):
            pe.wait_ge(setup_dve, 1)
            nc.tensor.matmul(ps_small[:, 0:2 * S], ones_row[0:1, :], proj_row[0:1, :],
                             start=True, stop=True).then_inc(proj_ps, 1)
            pe.wait_ge(posmap_ready, S)
            pe.wait_ge(pool_consts, 1)
            for s in range(S):
                ins = nc.tensor.transpose(ps_in[0][:, s * P:(s + 1) * P], posmap[:, s, :], ident[:, :])
            ins.then_inc(posmap_t, 1)
            pe.wait_ge(setup_done, 1)

            def average(ps, weights, srcs, done):
                for n, v in enumerate(srcs):
                    ins = nc.tensor.matmul(ps, weights, v, start=(n == 0), stop=(n == len(srcs) - 1))
                ins.then_inc(done, 1)

            def mix_chunk(b, c):
                n = b * CH + c
                pe.wait_ge(xl_ready, n + 1)
                for m in range(2):
                    if not is_zero(n):
                        pe.wait_ge(x1_done[m], n)
                    for s in (2 * m, 2 * m + 1):
                        ps = ps_mix[m][:, (s % 2) * CR * V:(s % 2 + 1) * CR * V]
                        nc.tensor.matmul(ps, mix_h[:, s, :], xh[:, s:CC:S], start=True, stop=False)
                        nc.tensor.matmul(ps, mix_h[:, s, :], xl[:, s:CC:S], start=False, stop=False)
                        ins = nc.tensor.matmul(ps, mix_l[:, s, :], xh[:, s:CC:S], start=False, stop=True)
                    ins.then_inc(mix_done[m], 1)

            def turn_in(b, c):
                n = b * CH + c
                pe.wait_ge(swapped[c], 64 * (b + 1))
                for u in range(2):
                    if not is_zero(n):
                        pe.wait_ge(in_kept, 2 * n - 1 + u)
                    for h in range(RG):
                        ins = nc.tensor.transpose(ps_in[u][:, h * P:(h + 1) * P],
                                                  x_swap[:, c % 2, RG * u + h, :, :].rearrange("p q c -> p (q c)"), ident[:, :])
                    ins.then_inc(in_turned, 1)

            def prep(b, i, after, prev):
                if i == 0 and after == 0:
                    pe.wait_ge(stats1_done, b + 1)
                    if not prev and not is_zero(b):
                        pe.wait_ge(shift2_ready, b)
                    average(mean1, inv256[:, :], [st1[:, half, :, 1] for half in range(2)], mean1_ps)
                    if prev:
                        turn_in(b - 1, 3)
                if i == 0 and after == 1:
                    pe.wait_ge(m2_ready, b + 1)
                    average(var1_ps, inv256[:, :], [m2[:, half, :] for half in range(2)], var1_in_ps)
                if i == 1 and after == 1:
                    pe.wait_ge(mean_rstd_ready, b + 1)
                    average(shift1_ps, mean_rstd[:, :, :, :].rearrange("p q g e -> p (q g e)"),
                            [minus_avg[:, :]], shift1_in_ps)
                if i == 2 and prev:
                    if after == 0:
                        pe.wait_ge(mv_ready, b)
                        average(mean2, group_avg[:, :, :, :].rearrange("p q g e -> p (q g e)"),
                                [mv[:, 0:1]], mean2_ps)
                    else:
                        pe.wait_ge(var_p_ready, b)
                        average(var2_ps, group_avg[:, :, :, :].rearrange("p q g e -> p (q g e)"),
                                [var_p[:, :]], var2_in_ps)
                if 2 <= i < 2 + CH and after == 1:
                    mix_chunk(b, i - 2)
                if i in TURN_STEP and after == 0:
                    turn_in(b, TURN_STEP[i])

            def finish(b):
                turn_in(b, 3)
                pe.wait_ge(mv_ready, b + 1)
                average(mean2, group_avg[:, :, :, :].rearrange("p q g e -> p (q g e)"), [mv[:, 0:1]], mean2_ps)
                pe.wait_ge(var_p_ready, b + 1)
                average(var2_ps, group_avg[:, :, :, :].rearrange("p q g e -> p (q g e)"), [var_p[:, :]], var2_in_ps)

            def turn_out(t):
                if not (isinstance(t, int) and t <= 1):
                    pe.wait_ge(out_staged, t - 1)
                for s in range(NS):
                    pe.wait_ge(total_ready[s], t)
                    for m in range(WS // 2):
                        ins = nc.tensor.transpose(ps_out[:, s * SW + m * P:s * SW + (m + 1) * P],
                                                  total[s][:, m * P:(m + 1) * P], ident[:, :])
                ins.then_inc(out_turned, 1)

            def convolve(t, s):
                pe.wait_ge(high_ready[s], t + 1)
                for w in (wh, wl):
                    for d in range(D):
                        nc.tensor.matmul(ps_conv[s][:, 0:SW], w[:, d, :], carry_h[s][:, :, d:d + J],
                                         start=(w is wh and d == 0), stop=False)
                pe.wait_ge(low_ready[s], t + 1)
                for d in range(D):
                    ins = nc.tensor.matmul(ps_conv[s][:, 0:SW], wh[:, d, :], carry_l[s][:, :, d:d + J],
                                           start=False, stop=(d == D - 1))
                ins.then_inc(conv_done[s], 1)

            def iteration(wave, it, b, prev):
                for i in range(STEPS):
                    t = (it + wave * ITERS) * STEPS + i
                    for s in range(NS):
                        convolve(t, s)
                        if s == 0 and not (i == 0 and is_zero(it)):
                            turn_out(t)
                        if b is not None:
                            prep(b, i, s, prev)

            for i in range(STEPS):
                for s in range(2):
                    prep(0, i, s, False)
            with pe.Fori(1, W) as b:
                for i in range(STEPS):
                    for s in range(2):
                        prep(b, i, s, True)
            finish(W - 1)
            iteration(0, 0, W, False)
            with pe.Fori(1, ITERS - 1) as it:
                iteration(0, it, it + W, True)
            iteration(0, ITERS - 1, B - 1, True)
            turn_out(H)
            finish(B - 1)
            iteration(1, 0, None, False)
            with pe.Fori(1, ITERS) as it:
                iteration(1, it, None, False)
            turn_out(2 * H)


_INS = ['x', 'L0_conv_attention_centers', 'L0_conv_attention_spreads', 'L0_conv_token_proj_n_bias', 'L1_conv_W']
_OUTS = [((16, 64, 128, 64), 'float32')]


def kernel(**inputs):
    import numpy as _np
    import concourse.bacc as _bacc
    from concourse import mybir as _mybir
    from concourse.bass_utils import run_bass_kernel_spmd as _run

    nc = _bacc.Bacc("TRN2", target_bir_lowering=False, num_devices=1)
    arrays, args = {}, []
    for name in _INS:
        a = _np.ascontiguousarray(inputs[name])
        arrays[f"in_{name}_dram"] = a
        args.append(nc.dram_tensor(f"in_{name}_dram", a.shape, _mybir.dt.from_np(a.dtype), kind="ExternalInput").ap())
    for i, (shape, dtype) in enumerate(_OUTS):
        dt = _mybir.dt.from_np(_np.dtype(dtype))
        args.append(nc.dram_tensor(f"out_{i}_dram", shape, dt, kind="ExternalOutput").ap())
    mix_and_scan_kernel(nc, *args)
    r = _run(nc, [arrays], core_ids=[0])
    return r.results[0]["out_0_dram"]
```

```python
import concourse.bass as bass
from concourse import mybir
from contextlib import ExitStack



def mix_and_scan_kernel(nc: bass.Bass, x: bass.AP, centers: bass.AP, spreads: bass.AP,
                        token_bias: bass.AP, conv_w: bass.AP, out: bass.AP):
    f32 = mybir.dt.float32
    f32r = mybir.dt.float32r
    i32 = mybir.dt.int32
    ALU = mybir.AluOpType
    ACT = mybir.ActivationFunctionType
    AX = mybir.AxisListType

    B, H, N, C = x.shape
    S = centers.shape[0]
    V = C // S
    K = conv_w.shape[0]
    PAD = (K - 1) // 2
    P = 128
    J = N // 2
    G = 32
    CG = C // G
    EPS = 1e-5
    D = PAD + 1
    EDGE = PAD // 2
    W = B // 2
    NS = 2
    WS = W // NS
    SW = WS * J
    STEPS = 8
    ITERS = H // STEPS
    CH = 4
    CR = H // CH
    CC = CR * C
    HR = CR // 2
    RG = 2
    GROUPS = STEPS // RG
    TU = 2 * CH
    HALF_COUNT = H // 2 * CG

    x_nat = x.rearrange("b h n c -> n b h c")
    out_pairs = out.rearrange("b h (j q) c -> b h j (q c)", q=2)

    with ExitStack() as ctx:
        def sb(name, shape, dt=f32):
            return ctx.enter_context(nc.sbuf_tensor(name, shape, dt))

        def pb(name):
            return ctx.enter_context(nc.psum_tensor(name, [P, 512], f32))

        def sem(name):
            return ctx.enter_context(nc.semaphore(name))

        x1_paired = sb("x1_paired", [P, H * W * J])
        rows = sb("rows", [P, 2, RG, W, J])
        x_sb = sb("x_sb", [P, 2, H * C])
        xs = sb("xs", [P, 2, CC])
        wh = sb("wh", [P, D, P], f32r)
        wl = sb("wl", [P, D, P], f32r)
        mix = sb("mix", [P, S, P])
        JP = J + 2 * EDGE
        carry_h = [sb(f"carry_h{s}", [P, WS, JP], f32r) for s in range(NS)]
        carry_l = [sb(f"carry_l{s}", [P, WS, JP], f32r) for s in range(NS)]
        carry = [sb(f"carry{s}", [P, SW]) for s in range(NS)]
        total = [sb(f"total{s}", [P, SW]) for s in range(NS)]
        staged = sb("staged", [P, 2, NS * SW])
        ident = sb("ident", [P, P])
        st1 = sb("st1", [P, 2, G, 3])
        dev = sb("dev", [P, 2, G])
        dev2 = sb("dev2", [P, 2, G])
        m2 = sb("m2", [P, 2, G])
        var1 = sb("var1", [P, G])
        std1 = sb("std1", [P, G])
        guess1 = sb("guess1", [P, G])
        square1 = sb("square1", [P, G])
        ratio1 = sb("ratio1", [P, G])
        rstd1 = sb("rstd1", [P, G])
        rstd1_c = sb("rstd1_c", [P, 2, G, CG])
        mean_rstd = sb("mean_rstd", [P, 2, G, CG])
        shift1 = sb("shift1", [P, 2])
        st2 = sb("st2", [P, 2 * CH, 6])
        mv = sb("mv", [P, 2])
        dev_c = sb("dev_c", [P, 1])
        var_p = sb("var_p", [P, 1])
        var2 = sb("var2", [P, 1])
        rstd2 = sb("rstd2", [P, B])
        shift2 = sb("shift2", [P, B])
        bias_col = sb("bias_col", [P, 1])
        half_power = sb("half_power", [P, 1])
        inv256 = sb("inv256", [P, P])
        minus_avg = sb("minus_avg", [P, 1])
        group_avg = sb("group_avg", [P, 2, G, CG])
        w_raw = x1_paired[:, 0:D * P].rearrange("p (d m) -> p d m", d=D)
        at = D * P

        def scratch(n):
            nonlocal at
            at += n
            return x1_paired[:, at - n:at]
        dist = scratch(P)
        dist_i = scratch(P).bitcast(i32)
        dist2 = scratch(P)
        score = scratch(S * P).rearrange("p (s n) -> p s n", s=S)
        lin = scratch(S * P).rearrange("p (s n) -> p s n", s=S)
        prob = scratch(S * P).rearrange("p (s n) -> p s n", s=S)
        posmap = scratch(S * P).rearrange("p (s n) -> p s n", s=S)
        att_row = scratch(2 * S)
        proj_row = scratch(2 * S)
        proj = scratch(2 * S)
        neg_max = scratch(S)
        peak = scratch(S)
        exp_sum = scratch(S)
        inv_sum = scratch(S)
        ones_row = scratch(P)
        group_of = scratch(G)

        ps_conv = [pb(f"ps_conv{s}") for s in range(NS)]
        ps_mix = [pb(f"ps_mix{n}") for n in range(2)]
        ps_in = [pb(f"ps_in{n}") for n in range(2)]
        ps_out = pb("ps_out")
        ps_small = pb("ps_small")
        mean1 = ps_small[:, 0:G]
        var1_ps = ps_small[:, G:2 * G]
        shift1_ps = ps_small[:, 64:65]
        mean2 = ps_small[:, 66:67]
        var2_ps = ps_small[:, 68:69]

        w_loaded = sem("w_loaded")
        small_loaded = sem("small_loaded")
        w_zeroed = sem("w_zeroed")
        w_high = sem("w_high")
        setup_dve = sem("setup_dve")
        consts = sem("consts")
        pool_chain = sem("pool_chain")
        pool_consts = sem("pool_consts")
        proj_ps = sem("proj_ps")
        score_ready = sem("score_ready")
        prob_ready = sem("prob_ready")
        posmap_ready = sem("posmap_ready")
        posmap_t = sem("posmap_t")
        setup_done = sem("setup_done")
        x_loaded = [[sem(f"x_loaded{e}_{c}") for c in range(CH)] for e in range(2)]
        stats1_done = sem("stats1_done")
        mean1_ps = sem("mean1_ps")
        dev_ready = sem("dev_ready")
        dev2_ready = sem("dev2_ready")
        m2_ready = sem("m2_ready")
        var1_in_ps = sem("var1_in_ps")
        var1_ready = sem("var1_ready")
        std1_ready = sem("std1_ready")
        guess1_ready = sem("guess1_ready")
        square1_ready = sem("square1_ready")
        ratio1_ready = sem("ratio1_ready")
        rstd1_ready = sem("rstd1_ready")
        rstd1_c_ready = sem("rstd1_c_ready")
        mean_rstd_ready = sem("mean_rstd_ready")
        shift1_in_ps = sem("shift1_in_ps")
        shift1_ready = sem("shift1_ready")
        xs_ready = sem("xs_ready")
        mix_done = [sem(f"mix_done{n}") for n in range(2)]
        x1_done = [sem(f"x1_done{n}") for n in range(2)]
        in_turned = sem("in_turned")
        in_kept = sem("in_kept")
        stats2_done = sem("stats2_done")
        mv_ready = sem("mv_ready")
        mean2_ps = sem("mean2_ps")
        dev_c_ready = sem("dev_c_ready")
        var_p_ready = sem("var_p_ready")
        var2_in_ps = sem("var2_in_ps")
        var2_ready = sem("var2_ready")
        rstd2_ready = sem("rstd2_ready")
        shift2_ready = sem("shift2_ready")
        rows_ready = sem("rows_ready")
        conv_done = [sem(f"conv_done{s}") for s in range(NS)]
        carry_ready = [sem(f"carry_ready{s}") for s in range(NS)]
        high_ready = [sem(f"high_ready{s}") for s in range(NS)]
        low_ready = [sem(f"low_ready{s}") for s in range(NS)]
        total_ready = [sem(f"total_ready{s}") for s in range(NS)]
        out_turned = sem("out_turned")
        out_staged = sem("out_staged")
        stored = [sem(f"stored{n}") for n in range(2)]

        def x1_unit(wave, b, c, u):
            if wave == 1:
                v = x1_paired[:, bass.ds(b * (H * J) + (c * CR + u * HR) * J, HR * J)]
                return v.rearrange("p (h j) -> p h j", j=J)
            v = x1_paired[:, :].rearrange("p (h w j) -> p h w j", w=W, j=J)
            v = v[:, c * CR + u * HR:c * CR + (u + 1) * HR, bass.ds(b, 1), :]
            return v.rearrange("p h w j -> p h (w j)")

        def x1_rows(wave, it, row, n, b0, nb):
            if wave == 0:
                v = x1_paired[:, bass.ds(it * (STEPS * W * J) + row * W * J, n * W * J)]
                return v.rearrange("p (h w j) -> p h w j", h=n, w=W)[:, :, b0:b0 + nb, :]
            v = x1_paired[:, :].rearrange("p (w h j) -> p h w j", w=W, j=J)
            return v[:, bass.ds(it * STEPS + row, n), b0:b0 + nb, :]

        def alone(eng, done):
            eng.wait_ge(done, 1)

        def held(eng, n):
            return n if isinstance(n, int) else eng.to_reg(n)

        def is_zero(n):
            return isinstance(n, int) and n == 0

        def is_last(it):
            return isinstance(it, int) and it == ITERS - 1

        block = ctx.enter_context(nc.Block())

        @block.sync
        def _(sp):
            def load_chunk(b, e, c):
                if not (isinstance(b, int) and b < 2):
                    turned = held(sp, TU * b - 2 * TU + 2 * c + 2)
                    alone(sp, w_zeroed)
                    sp.wait_ge(in_turned, turned)
                sp.dma_start(x_sb[:, e, c * CC:(c + 1) * CC].rearrange("n (h c) -> n h c", c=C),
                             x_nat[:, bass.ds(b, 1), c * CR:(c + 1) * CR, :].rearrange("n b h c -> n (b h) c")
                             ).then_inc(x_loaded[e][c], 16)

            for c in range(CH):
                load_chunk(0, 0, c)
            sp.wait_ge(w_zeroed, 1)
            for q in range(2):
                for o in range(2):
                    ds = [d for d in range(D) if 0 <= 2 * d + q - o < K]
                    k0 = 2 * ds[0] + q - o
                    sp.dma_start(w_raw[q * C:(q + 1) * C, ds[0]:ds[-1] + 1, o * C:(o + 1) * C],
                                 conv_w[k0:k0 + 2 * len(ds) - 1:2, :, :].rearrange("k c o -> c k o")
                                 ).then_inc(w_loaded, 16)
            for c in range(CH):
                load_chunk(1, 1, c)
            with sp.Fori(1, B // 2) as pair:
                for e in range(2):
                    for c in range(CH):
                        load_chunk(2 * pair + e, e, c)

        @block.gpsimd
        def _(pool):
            nc.gpsimd.memset(ident[:, :], 0.0).then_inc(pool_chain, 1)
            nc.gpsimd.memset(group_of, 0.0).then_inc(pool_chain, 1)
            pool.wait_ge(pool_chain, 2)
            nc.gpsimd.affine_select(out=ident[:, :], in_=ident[:, :], compare_op=ALU.not_equal, fill=1.0,
                                    base=0, pattern=[[-1, P]], channel_multiplier=1).then_inc(pool_consts, 1)
            n = 2
            for q in range(2):
                for e in range(CG):
                    nc.gpsimd.affine_select(out=group_of, in_=group_of, compare_op=ALU.not_equal,
                                            fill=1.0 / (2 * CG), base=-(q * C + e), pattern=[[-CG, G]],
                                            channel_multiplier=1).then_inc(pool_chain, 1)
                    n += 1
                    pool.wait_ge(pool_chain, n)
            for q in range(2):
                for e in range(CG):
                    nc.gpsimd.tensor_copy(group_avg[:, q, :, e], group_of).then_inc(pool_consts, 1)
            nc.gpsimd.iota(dist_i, pattern=[[1, N]], base=0,
                           channel_multiplier=-1).then_inc(pool_consts, 1)

            def spread_rstd1(b):
                ready, read, own = held(pool, b + 1), held(pool, b), held(pool, 2 * b + 2)
                alone(pool, consts)
                pool.wait_ge(rstd1_ready, ready)
                if not is_zero(b):
                    pool.wait_ge(mean_rstd_ready, read)
                for q in range(2):
                    nc.gpsimd.tensor_copy(rstd1_c[:, q, :, :],
                                          rstd1[:, :].unsqueeze(2).to_broadcast([P, G, CG])
                                          ).then_inc(rstd1_c_ready, 1)
                pool.wait_ge(rstd1_c_ready, own)

            def scale_chunk(b, e, c):
                n = b * CH + c
                if not (isinstance(b, int) and n < 2):
                    for m in range(2):
                        pool.wait_ge(mix_done[m], n - 1)
                src = x_sb[:, e, c * CC:(c + 1) * CC].rearrange("p (h c) -> p h c", c=C)
                r = rstd1_c[:, 0, :, :].rearrange("p g e -> p (g e)").unsqueeze(1).to_broadcast([P, CR, C])
                nc.gpsimd.tensor_tensor(xs[:, c % 2, :].rearrange("p (h c) -> p h c", c=C), src, r,
                                        ALU.mult).then_inc(xs_ready, 1)

            def rstd2_of(b):
                pool.wait_ge(var2_ready, b + 1)
                nc.gpsimd.tensor_tensor(rstd2[:, bass.ds(b, 1)], var2[:, :], half_power[:, 0:1],
                                        ALU.pow).then_inc(rstd2_ready, 1)

            def prep(b, e, i, prev, more):
                if i == 5 and prev:
                    rstd2_of(b - 1)
                if i % 2 == 1 and i < STEPS - 1:
                    scale_chunk(b, e, (i + 1) // 2)
                if i == 6 and more:
                    spread_rstd1(b + 1)
                if i == 7 and more:
                    scale_chunk(b + 1, 1 - e, 0)

            def add_carry(wave, it, i, s):
                t = (it + wave * ITERS) * STEPS + i
                pool.wait_ge(carry_ready[s], t + 1)
                if not is_zero(t):
                    pool.wait_ge(out_turned, t)
                nc.gpsimd.tensor_tensor(total[s][:, :].rearrange("p (w j) -> p w j", w=WS),
                                        x1_rows(wave, it, i, 1, s * WS, WS)[:, 0, :, :],
                                        carry[s][:, :].rearrange("p (w j) -> p w j", w=WS),
                                        ALU.add).then_inc(total_ready[s], 1)

            def iteration(wave, it, b, e, prev, more):
                for i in range(STEPS):
                    for s in range(NS):
                        add_carry(wave, it, i, s)
                    if b is not None:
                        prep(b, e, i, prev, more)

            pool.wait_ge(consts, 1)
            spread_rstd1(0)
            scale_chunk(0, 0, 0)
            for e in range(2):
                for i in range(STEPS):
                    prep(e, e, i, e > 0, True)
            with pool.Fori(1, W // 2) as pair:
                for e in range(2):
                    for i in range(STEPS):
                        prep(2 * pair + e, e, i, True, True)
            rstd2_of(W - 1)
            for e in range(2):
                iteration(0, e, W + e, e, e > 0, True)
            with pool.Fori(1, ITERS // 2 - 1) as pair:
                for e in range(2):
                    iteration(0, 2 * pair + e, 2 * pair + (W + e), e, True, True)
            for e in range(2):
                iteration(0, ITERS - 2 + e, B - 2 + e, e, True, e == 0)
            rstd2_of(B - 1)
            with pool.Fori(0, ITERS) as it:
                iteration(1, it, None, None, False, False)

        @block.scalar
        def _(act):
            act.dma_start(att_row[0:1, 0:S], centers.rearrange("s a -> a s")).then_inc(small_loaded, 16)
            act.dma_start(att_row[0:1, S:2 * S], spreads.rearrange("s a -> a s")).then_inc(small_loaded, 16)
            act.dma_start(bias_col[:, :], token_bias.rearrange("a n e -> n (a e)")).then_inc(small_loaded, 16)
            for s in range(S):
                act.wait_ge(score_ready, s + 1)
                nc.scalar.activation(prob[:, s, :], score[:, s, :], ACT.Exp, bias=neg_max[:, s:s + 1],
                                     accum_out=exp_sum[:, s:s + 1]).then_inc(prob_ready, 1)

            def std1_of(b):
                act.wait_ge(var1_ready, b + 1)
                nc.scalar.activation(std1[:, :], var1[:, :], ACT.Sqrt).then_inc(std1_ready, 1)

            def keep_in(b, e, wave, bw, c, u, free):
                n = b * CH + c
                act.wait_ge(shift1_ready, b + 1)
                half = held(act, 2 * n + u + 1)
                alone(act, setup_done)
                if free is not None:
                    for s in range(NS):
                        act.wait_ge(total_ready[s], free)
                act.wait_ge(in_turned, half)
                dst = x1_unit(wave, bw, c, u)
                for r in range(2):
                    src = ps_in[u][r * C:(r + 1) * C, :].rearrange("p (k j q) -> p q k j", k=HR // 2, q=2)
                    for q in range(2):
                        ins = nc.scalar.activation(dst[q * C:(q + 1) * C, r:HR:2, :], src[:, q, :, :],
                                                   ACT.Identity, bias=shift1[r * C:(r + 1) * C, e:e + 1])
                ins.then_inc(in_kept, 1)

            def prep(b, e, wave, bw, i, prev, it):
                if i < 3 and prev:
                    c, u = (i + 5) // 2, (i + 5) % 2
                    keep_in(b - 1, 1 - e, wave, bw - 1, c, u, None if it is None else (it - 1) * STEPS + 2 * c + 2)
                if i >= 3:
                    c, u = (i - 3) // 2, (i - 3) % 2
                    keep_in(b, e, wave, bw, c, u, None if it is None else it * STEPS + 2 * c + 2)

            def finish(b, e, wave, bw, free):
                for n in range(5, TU):
                    keep_in(b, e, wave, bw, n // 2, n % 2, free)

            def norm_rows(wave, it, g, w):
                t = (it + wave * ITERS) * STEPS + g * RG
                if not (isinstance(t, int) and t < 2 * RG):
                    used = held(act, t - RG)
                    alone(act, setup_done)
                    for s in range(NS):
                        act.wait_ge(carry_ready[s], used)
                b = wave * W + w
                nc.scalar.activation(rows[:, g % 2, :, w, :], x1_rows(wave, it, g * RG, RG, w, 1)[:, :, 0, :],
                                     ACT.Identity, scale=rstd2[:, b:b + 1],
                                     bias=shift2[:, b:b + 1]).then_inc(rows_ready, 1)

            def stage_out(t, buf):
                act.wait_ge(out_turned, t)
                if not (isinstance(t, int) and t <= 2):
                    act.wait_ge(stored[buf], (t - 1 - buf) * 16)
                nc.scalar.activation(staged[:, buf, :], ps_out[:, :], ACT.Copy).then_inc(out_staged, 1)

            def store_row(wave, h, t, buf):
                act.wait_ge(out_staged, t)
                src = staged[:, buf, :].rearrange("p (m f) -> p m f", f=P)
                for e in range(2):
                    dst = out_pairs[wave * W + e:(wave + 1) * W:2, bass.ds(h, 1), :, :]
                    act.dma_start(dst.rearrange("m h j f -> (h j) m f"),
                                  src[e * J:(e + 1) * J, :, :]).then_inc(stored[buf], 16)

            def iteration(wave, it, b, e, prev, more):
                first, last = is_zero(it), is_last(it)
                for i in range(STEPS):
                    t = (it + wave * ITERS) * STEPS + i
                    begins = first and i == 0
                    for s in range(NS):
                        if not (last and i == STEPS - 1):
                            act.wait_ge(carry_ready[s], t + 1)
                            nc.scalar.activation(carry_h[s][:, :, EDGE:EDGE + J],
                                                 carry[s][:, :].rearrange("p (w j) -> p w j", w=WS),
                                                 ACT.Copy).then_inc(high_ready[s], 1)
                        if s == 0 and not begins:
                            stage_out(t, (i + 1) % 2)
                        if s == 1 and not begins:
                            store_row(wave, it * STEPS + i - 1, t, (i + 1) % 2)
                        g = i // RG + 1
                        if not (last and g == GROUPS):
                            for k in range(2):
                                norm_rows(wave, it + g // GROUPS, g % GROUPS, (i % RG) * 2 * NS + 2 * s + k)
                        if s == 1 and i == 6 and more:
                            std1_of(b + 1)
                    if b is not None:
                        prep(b, e, 1, it, i, prev, it)

            def alone_prep(b, e, prev):
                for i in range(STEPS):
                    if i == 6:
                        std1_of(b + 1)
                    prep(b, e, 0, b, i, prev, None)

            act.wait_ge(setup_done, 1)
            std1_of(0)
            for e in range(2):
                alone_prep(e, e, e > 0)
            with act.Fori(1, W // 2) as pair:
                for e in range(2):
                    alone_prep(2 * pair + e, e, True)
            finish(W - 1, 1, 0, W - 1, None)
            act.wait_ge(shift2_ready, W)
            for w in range(W):
                norm_rows(0, 0, 0, w)
            for e in range(2):
                iteration(0, e, W + e, e, e > 0, True)
            with act.Fori(1, ITERS // 2 - 1) as pair:
                for e in range(2):
                    iteration(0, 2 * pair + e, 2 * pair + (W + e), e, True, True)
            for e in range(2):
                iteration(0, ITERS - 2 + e, B - 2 + e, e, True, e == 0)
            finish(B - 1, 1, 1, W - 1, H)
            stage_out(H, 1)
            store_row(0, H - 1, H, 1)
            act.wait_ge(shift2_ready, B)
            for w in range(W):
                norm_rows(1, 0, 0, w)
            iteration(1, 0, None, None, False, False)
            with act.Fori(1, ITERS - 1) as it:
                iteration(1, it, None, None, False, False)
            iteration(1, ITERS - 1, None, None, False, False)
            stage_out(2 * H, 1)
            store_row(1, H - 1, 2 * H, 1)
            for n in range(2):
                act.wait_ge(stored[n], 2 * H // 2 * 32)

        @block.vector
        def _(dve):
            nc.vector.memset(w_raw, 0.0).then_inc(w_zeroed, 1)
            nc.vector.memset(half_power[:, :], -0.5).then_inc(consts, 1)
            nc.vector.memset(ones_row, 1.0)
            nc.vector.memset(inv256[:, :], 1.0 / (2 * P))
            nc.vector.memset(minus_avg[:, :], -1.0 / P)
            for s in range(NS):
                nc.vector.memset(carry_h[s][:, :, :].bitcast(f32), 0.0).then_inc(high_ready[s], 1)
                nc.vector.memset(carry_l[s][:, :, :].bitcast(f32), 0.0).then_inc(low_ready[s], 1)

            def stats1(b, e, half, first, count):
                for c in (2 * half, 2 * half + 1):
                    dve.wait_ge(x_loaded[e][c], 8 * (b - e) + 16)
                v = x_sb[:, e, 2 * half * CC:2 * (half + 1) * CC]
                v = v.rearrange("p (h m g e) -> p m h e g", m=G // 2, g=2, e=CG)
                for m in range(first, first + count):
                    ins = nc.vector.bn_stats(st1[:, half, 2 * m:2 * m + 2, :].rearrange("p g k -> p (g k)"),
                                             v[:, m, :, :, :])
                if half == 1 and first + count == G // 2:
                    ins.then_inc(stats1_done, 1)

            for half in range(2):
                stats1(0, 0, half, 0, G // 2)

            dve.wait_ge(small_loaded, 48)
            dve.wait_ge(pool_consts, 2 + 2 * CG)
            nc.vector.tensor_tensor(proj_row[0:1, 0:S], att_row[0:1, 0:S], att_row[0:1, S:2 * S], ALU.mult)
            nc.vector.tensor_scalar(proj_row[0:1, S:2 * S], att_row[0:1, S:2 * S], -0.5, None,
                                    ALU.mult).then_inc(setup_dve, 1)
            nc.vector.tensor_copy(dist, dist_i).then_inc(setup_dve, 1)
            dve.wait_ge(setup_dve, 2)
            nc.vector.tensor_tensor(dist2, dist, dist, ALU.mult).then_inc(setup_dve, 1)
            dve.wait_ge(proj_ps, 1)
            nc.vector.tensor_copy(proj, ps_small[:, 0:2 * S]).then_inc(setup_dve, 1)
            dve.wait_ge(setup_dve, 4)
            for s in range(S):
                nc.vector.tensor_scalar(lin[:, s, :], dist, proj[:, s:s + 1], None, ALU.mult).then_inc(setup_dve, 1)
            dve.wait_ge(setup_dve, 4 + S)
            for s in range(S):
                nc.vector.scalar_tensor_tensor(score[:, s, :], dist2, proj[:, S + s:S + s + 1], lin[:, s, :],
                                               ALU.mult, ALU.add).then_inc(setup_dve, 1)
            dve.wait_ge(setup_dve, 4 + 2 * S)
            nc.vector.reduce_max(peak, score, AX.X).then_inc(setup_dve, 1)
            dve.wait_ge(setup_dve, 5 + 2 * S)
            nc.vector.tensor_scalar(neg_max, peak, -1.0, None, ALU.mult).then_inc(score_ready, S)
            dve.wait_ge(prob_ready, S)
            nc.vector.reciprocal(inv_sum, exp_sum).then_inc(setup_dve, 1)
            dve.wait_ge(setup_dve, 6 + 2 * S)
            for s in range(S):
                nc.vector.tensor_scalar(posmap[:, s, :], prob[:, s, :], inv_sum[:, s:s + 1], None,
                                        ALU.mult).then_inc(posmap_ready, 1)
            dve.wait_ge(w_loaded, 64)
            nc.vector.tensor_copy(wh[:, :, :], w_raw).then_inc(w_high, 1)
            dve.wait_ge(w_high, 1)
            nc.vector.tensor_tensor(wl[:, :, :], w_raw, wh[:, :, :].bitcast(f32), ALU.subtract)
            dve.wait_ge(posmap_t, 1)
            turned = ps_in[0][:, :].rearrange("p (s m) -> p s m", s=S)
            nc.vector.tensor_copy(mix[:, :, :], turned).then_inc(setup_done, 1)

            def spread(row):
                return row.unsqueeze(1).unsqueeze(3).to_broadcast([P, 2, G, CG])

            def deviations1(b):
                dve.wait_ge(mean1_ps, b + 1)
                nc.vector.tensor_tensor(dev[:, :, :], st1[:, :, :, 1],
                                        mean1.unsqueeze(1).to_broadcast([P, 2, G]),
                                        ALU.subtract).then_inc(dev_ready, 1)
                dve.wait_ge(dev_ready, b + 1)
                nc.vector.tensor_tensor(dev2[:, :, :], dev[:, :, :], dev[:, :, :], ALU.mult).then_inc(dev2_ready, 1)
                dve.wait_ge(dev2_ready, b + 1)
                nc.vector.scalar_tensor_tensor(m2[:, :, :], dev2[:, :, :], float(HALF_COUNT), st1[:, :, :, 2],
                                               ALU.mult, ALU.add).then_inc(m2_ready, 1)

            def variance1(b):
                dve.wait_ge(var1_in_ps, b + 1)
                nc.vector.tensor_scalar(var1[:, :], var1_ps, 1.0 / HALF_COUNT, EPS, ALU.mult,
                                        ALU.add).then_inc(var1_ready, 1)

            def rstd1_of(b):
                dve.wait_ge(std1_ready, b + 1)
                nc.vector.reciprocal(guess1[:, :], std1[:, :]).then_inc(guess1_ready, 1)
                dve.wait_ge(guess1_ready, b + 1)
                nc.vector.scalar_tensor_tensor(square1[:, :], guess1[:, :], -0.5, guess1[:, :],
                                               ALU.mult, ALU.mult).then_inc(square1_ready, 1)
                dve.wait_ge(square1_ready, b + 1)
                nc.vector.tensor_tensor(ratio1[:, :], square1[:, :], var1[:, :], ALU.mult).then_inc(ratio1_ready, 1)
                dve.wait_ge(ratio1_ready, b + 1)
                nc.vector.scalar_tensor_tensor(rstd1[:, :], ratio1[:, :], 1.5, guess1[:, :],
                                               ALU.add, ALU.mult).then_inc(rstd1_ready, 1)

            def mean_rstd1(b):
                dve.wait_ge(rstd1_c_ready, 2 * b + 2)
                nc.vector.tensor_tensor(mean_rstd[:, :, :, :], spread(mean1), rstd1_c[:, :, :, :],
                                        ALU.mult).then_inc(mean_rstd_ready, 1)

            def keep_shift1(b, e):
                dve.wait_ge(shift1_in_ps, b + 1)
                if not (isinstance(b, int) and b < 2):
                    dve.wait_ge(in_kept, TU * b - TU)
                nc.vector.tensor_copy(shift1[:, e:e + 1], shift1_ps).then_inc(shift1_ready, 1)

            def mix_to_x1(b, e, c, m):
                dve.wait_ge(mix_done[m], b * CH + c + 1)
                v = x_sb[:, e, c * CC:(c + 1) * CC].rearrange("p (n s) -> p s n", s=S)[:, 2 * m:2 * m + 2, :]
                nc.vector.scalar_tensor_tensor(v, ps_mix[m][:, :].rearrange("p (s n) -> p s n", s=2),
                                               bias_col[:, 0:1], v, ALU.add, ALU.add).then_inc(x1_done[m], 1)

            def stats2(b, wave, bw, c, u):
                if c == 0 and u == 0 and not is_zero(b):
                    dve.wait_ge(mv_ready, b)
                dve.wait_ge(in_kept, 2 * (b * CH + c) + u + 1)
                nc.vector.bn_stats(st2[:, 2 * c + u, :], x1_unit(wave, bw, c, u)).then_inc(stats2_done, 1)

            def moments2(b):
                seen = held(dve, TU * b + TU)
                alone(dve, consts)
                dve.wait_ge(stats2_done, seen)
                nc.vector.bn_aggr(mv[:, :], st2[:, :, :].rearrange("p n k -> p (n k)")).then_inc(mv_ready, 1)

            def deviations2(b):
                dve.wait_ge(mean2_ps, b + 1)
                nc.vector.tensor_tensor(dev_c[:, :], mv[:, 0:1], mean2, ALU.subtract).then_inc(dev_c_ready, 1)
                dve.wait_ge(dev_c_ready, b + 1)
                nc.vector.scalar_tensor_tensor(var_p[:, :], dev_c[:, :], dev_c[:, 0:1], mv[:, 1:2],
                                               ALU.mult, ALU.add).then_inc(var_p_ready, 1)

            def variance2(b):
                dve.wait_ge(var2_in_ps, b + 1)
                nc.vector.tensor_scalar(var2[:, :], var2_ps, EPS, None, ALU.add).then_inc(var2_ready, 1)

            def shift2_of(b):
                dve.wait_ge(rstd2_ready, b + 1)
                nc.vector.scalar_tensor_tensor(shift2[:, bass.ds(b, 1)], mean2, -1.0, rstd2[:, bass.ds(b, 1)],
                                               ALU.mult, ALU.mult).then_inc(shift2_ready, 1)

            def prep(b, e, wave, bw, i, gap, prev, more):
                if gap == 0 and (i > 0 or prev):
                    if i > 0:
                        mix_to_x1(b, e, (i - 1) // 2, (i - 1) % 2)
                    else:
                        mix_to_x1(b - 1, 1 - e, 3, 1)
                if i == 6 and gap == 0 and prev:
                    shift2_of(b - 1)
                if i == 6 and gap == 1 and more:
                    deviations1(b + 1)
                if i == 6 and gap == 3 and more:
                    variance1(b + 1)
                if i == 7 and gap == 0 and more:
                    rstd1_of(b + 1)
                if i == 7 and gap == 2 and more:
                    mean_rstd1(b + 1)
                if i == 7 and gap == 3 and more:
                    keep_shift1(b + 1, 1 - e)
                if gap == 1:
                    if i >= 4:
                        stats2(b, wave, bw, (i - 4) // 2, (i - 4) % 2)
                    elif prev:
                        stats2(b - 1, wave, bw - 1, (i + 4) // 2, (i + 4) % 2)
                if i == 3 and gap == 3 and prev:
                    moments2(b - 1)
                if i == 4 and gap == 3 and prev:
                    deviations2(b - 1)
                if i == 5 and gap == 3 and prev:
                    variance2(b - 1)
                if more and i < 4:
                    stats1(b + 1, 1 - e, 0, 4 * i + gap, 1)
                if more and 4 <= i < 6:
                    stats1(b + 1, 1 - e, 1, 8 * (i - 4) + 2 * gap, 2)

            def finish(b, e, wave, bw):
                mix_to_x1(b, e, 3, 1)
                for n in range(4, TU):
                    stats2(b, wave, bw, n // 2, n % 2)
                moments2(b)
                deviations2(b)
                variance2(b)
                shift2_of(b)

            def iteration(wave, it, b, e, prev, more):
                last = is_last(it)
                for i in range(STEPS):
                    t = (it + wave * ITERS) * STEPS + i
                    for s in range(NS):
                        dve.wait_ge(conv_done[s], t + 1)
                        if i % RG == 0:
                            dve.wait_ge(rows_ready, W // RG * t + W)
                        if not is_zero(t):
                            dve.wait_ge(total_ready[s], t)
                        nc.vector.scalar_tensor_tensor(
                            carry[s][:, :], ps_conv[s][:, 0:SW], 0.0,
                            rows[:, (i // RG) % 2, i % RG, s * WS:(s + 1) * WS, :].rearrange("p w j -> p (w j)"),
                            ALU.max, ALU.add).then_inc(carry_ready[s], 1)
                        if b is not None:
                            prep(b, e, 1, it, i, 2 * s, prev, more)
                        if not (last and i == STEPS - 1):
                            dve.wait_ge(high_ready[s], t + 2)
                            nc.vector.tensor_tensor(carry_l[s][:, :, EDGE:EDGE + J],
                                                    carry[s][:, :].rearrange("p (w j) -> p w j", w=WS),
                                                    carry_h[s][:, :, EDGE:EDGE + J].bitcast(f32),
                                                    ALU.subtract).then_inc(low_ready[s], 1)
                        if b is not None:
                            prep(b, e, 1, it, i, 2 * s + 1, prev, more)

            def alone_prep(b, e, prev):
                for i in range(STEPS):
                    for gap in range(4):
                        prep(b, e, 0, b, i, gap, prev, True)

            deviations1(0)
            variance1(0)
            rstd1_of(0)
            mean_rstd1(0)
            keep_shift1(0, 0)
            for e in range(2):
                alone_prep(e, e, e > 0)
            with dve.Fori(1, W // 2) as pair:
                for e in range(2):
                    alone_prep(2 * pair + e, e, True)
            finish(W - 1, 1, 0, W - 1)
            for e in range(2):
                iteration(0, e, W + e, e, e > 0, True)
            with dve.Fori(1, ITERS // 2 - 1) as pair:
                for e in range(2):
                    iteration(0, 2 * pair + e, 2 * pair + (W + e), e, True, True)
            for e in range(2):
                iteration(0, ITERS - 2 + e, B - 2 + e, e, True, e == 0)
            for s in range(NS):
                nc.vector.memset(carry_h[s][:, :, :].bitcast(f32), 0.0).then_inc(high_ready[s], 1)
                nc.vector.memset(carry_l[s][:, :, :].bitcast(f32), 0.0).then_inc(low_ready[s], 1)
            finish(B - 1, 1, 1, W - 1)
            with dve.Fori(0, ITERS - 1) as it:
                iteration(1, it, None, None, False, False)
            iteration(1, ITERS - 1, None, None, False, False)

        @block.tensor
        def _(pe):
            pe.wait_ge(setup_dve, 1)
            nc.tensor.matmul(ps_small[:, 0:2 * S], ones_row[0:1, :], proj_row[0:1, :],
                             start=True, stop=True).then_inc(proj_ps, 1)
            pe.wait_ge(posmap_ready, S)
            pe.wait_ge(pool_consts, 1)
            for s in range(S):
                ins = nc.tensor.transpose(ps_in[0][:, s * P:(s + 1) * P], posmap[:, s, :], ident[:, :])
            ins.then_inc(posmap_t, 1)
            pe.wait_ge(setup_done, 1)

            def average(ps, weights, srcs, done):
                for n, v in enumerate(srcs):
                    ins = nc.tensor.matmul(ps, weights, v, start=(n == 0), stop=(n == len(srcs) - 1))
                ins.then_inc(done, 1)

            def mix_bank(b, c, m):
                n = b * CH + c
                pe.wait_ge(xs_ready, n + 1)
                if not is_zero(n):
                    pe.wait_ge(x1_done[m], n)
                for s in (2 * m, 2 * m + 1):
                    ins = nc.tensor.matmul(ps_mix[m][:, (s % 2) * CR * V:(s % 2 + 1) * CR * V],
                                           mix[:, s, :], xs[:, c % 2, s:CC:S], start=True, stop=True)
                ins.then_inc(mix_done[m], 1)

            def turn_in(b, e, c, u):
                n = b * CH + c
                for m in range(2):
                    pe.wait_ge(x1_done[m], n + 1)
                if not is_zero(n):
                    pe.wait_ge(in_kept, 2 * n - 1 + u)
                for k in range(HR // 2):
                    at = c * CC + (u * HR + 2 * k) * C
                    ins = nc.tensor.transpose(ps_in[u][:, k * P:(k + 1) * P], x_sb[:, e, at:at + P], ident[:, :])
                ins.then_inc(in_turned, 1)

            def mean1_of(b):
                pe.wait_ge(stats1_done, b + 1)
                average(mean1, inv256[:, :], [st1[:, half, :, 1] for half in range(2)], mean1_ps)

            def var1_of(b):
                pe.wait_ge(m2_ready, b + 1)
                average(var1_ps, inv256[:, :], [m2[:, half, :] for half in range(2)], var1_in_ps)

            def shift1_of(b):
                pe.wait_ge(mean_rstd_ready, b + 1)
                average(shift1_ps, mean_rstd[:, :, :, :].rearrange("p q g e -> p (q g e)"),
                        [minus_avg[:, :]], shift1_in_ps)

            def mean2_of(b):
                pe.wait_ge(mv_ready, b + 1)
                average(mean2, group_avg[:, :, :, :].rearrange("p q g e -> p (q g e)"), [mv[:, 0:1]], mean2_ps)

            def var2_of(b):
                pe.wait_ge(var_p_ready, b + 1)
                average(var2_ps, group_avg[:, :, :, :].rearrange("p q g e -> p (q g e)"), [var_p[:, :]], var2_in_ps)

            def prep(b, e, i, after, prev, more):
                if after == 0:
                    if i == 4 and prev:
                        mean2_of(b - 1)
                    if i == 6 and more:
                        if not is_zero(b):
                            pe.wait_ge(shift2_ready, b)
                        mean1_of(b + 1)
                    if i < 3 and prev:
                        turn_in(b - 1, 1 - e, (i + 5) // 2, (i + 5) % 2)
                    if i >= 3:
                        turn_in(b, e, (i - 3) // 2, (i - 3) % 2)
                else:
                    if i == 4 and prev:
                        var2_of(b - 1)
                    if i == 6 and more:
                        var1_of(b + 1)
                    mix_bank(b, i // 2, i % 2)
                    if i == 7 and more:
                        shift1_of(b + 1)

            def finish(b, e):
                for n in range(5, TU):
                    turn_in(b, e, n // 2, n % 2)
                mean2_of(b)
                var2_of(b)

            def turn_out(t):
                if not (isinstance(t, int) and t <= 1):
                    pe.wait_ge(out_staged, t - 1)
                for s in range(NS):
                    pe.wait_ge(total_ready[s], t)
                    for m in range(WS // 2):
                        ins = nc.tensor.transpose(ps_out[:, s * SW + m * P:s * SW + (m + 1) * P],
                                                  total[s][:, m * P:(m + 1) * P], ident[:, :])
                ins.then_inc(out_turned, 1)

            def convolve(t, s):
                pe.wait_ge(high_ready[s], t + 1)
                for w in (wh, wl):
                    for d in range(D):
                        nc.tensor.matmul(ps_conv[s][:, 0:SW], w[:, d, :], carry_h[s][:, :, d:d + J],
                                         start=(w is wh and d == 0), stop=False)
                pe.wait_ge(low_ready[s], t + 1)
                for d in range(D):
                    ins = nc.tensor.matmul(ps_conv[s][:, 0:SW], wh[:, d, :], carry_l[s][:, :, d:d + J],
                                           start=False, stop=(d == D - 1))
                ins.then_inc(conv_done[s], 1)

            def iteration(wave, it, b, e, prev, more):
                for i in range(STEPS):
                    t = (it + wave * ITERS) * STEPS + i
                    for s in range(NS):
                        convolve(t, s)
                        if s == 0 and not (i == 0 and is_zero(it)):
                            turn_out(t)
                        if b is not None:
                            prep(b, e, i, s, prev, more)

            def alone_prep(b, e, prev):
                for i in range(STEPS):
                    for after in range(2):
                        prep(b, e, i, after, prev, True)

            mean1_of(0)
            var1_of(0)
            shift1_of(0)
            for e in range(2):
                alone_prep(e, e, e > 0)
            with pe.Fori(1, W // 2) as pair:
                for e in range(2):
                    alone_prep(2 * pair + e, e, True)
            finish(W - 1, 1)
            for e in range(2):
                iteration(0, e, W + e, e, e > 0, True)
            with pe.Fori(1, ITERS // 2 - 1) as pair:
                for e in range(2):
                    iteration(0, 2 * pair + e, 2 * pair + (W + e), e, True, True)
            for e in range(2):
                iteration(0, ITERS - 2 + e, B - 2 + e, e, True, e == 0)
            turn_out(H)
            finish(B - 1, 1)
            iteration(1, 0, None, None, False, False)
            with pe.Fori(1, ITERS) as it:
                iteration(1, it, None, None, False, False)
            turn_out(2 * H)


_INS = ['x', 'L0_conv_attention_centers', 'L0_conv_attention_spreads', 'L0_conv_token_proj_n_bias', 'L1_conv_W']
_OUTS = [((16, 64, 128, 64), 'float32')]


def kernel(**inputs):
    import numpy as _np
    import concourse.bacc as _bacc
    from concourse import mybir as _mybir
    from concourse.bass_utils import run_bass_kernel_spmd as _run

    nc = _bacc.Bacc("TRN2", target_bir_lowering=False, num_devices=1)
    arrays, args = {}, []
    for name in _INS:
        a = _np.ascontiguousarray(inputs[name])
        arrays[f"in_{name}_dram"] = a
        args.append(nc.dram_tensor(f"in_{name}_dram", a.shape, _mybir.dt.from_np(a.dtype), kind="ExternalInput").ap())
    for i, (shape, dtype) in enumerate(_OUTS):
        dt = _mybir.dt.from_np(_np.dtype(dtype))
        args.append(nc.dram_tensor(f"out_{i}_dram", shape, dt, kind="ExternalOutput").ap())
    mix_and_scan_kernel(nc, *args)
    r = _run(nc, [arrays], core_ids=[0])
    return r.results[0]["out_0_dram"]
```

```python
import concourse.bass as bass
from concourse import mybir
from contextlib import ExitStack



def mix_and_scan_kernel(nc: bass.Bass, x: bass.AP, centers: bass.AP, spreads: bass.AP,
                        token_bias: bass.AP, conv_w: bass.AP, out: bass.AP):
    f32 = mybir.dt.float32
    f32r = mybir.dt.float32r
    i32 = mybir.dt.int32
    ALU = mybir.AluOpType
    ACT = mybir.ActivationFunctionType
    AX = mybir.AxisListType

    B, H, N, C = x.shape
    S = centers.shape[0]
    V = C // S
    K = conv_w.shape[0]
    PAD = (K - 1) // 2
    P = 128
    J = N // 2
    G = 32
    CG = C // G
    EPS = 1e-5
    D = PAD + 1
    EDGE = PAD // 2
    W = B // 2
    NS = 2
    WS = W // NS
    SW = WS * J
    STEPS = 8
    ITERS = H // STEPS
    CH = 4
    CR = H // CH
    CC = CR * C
    HR = CR // 2
    RG = 2
    GROUPS = STEPS // RG
    TU = 2 * CH
    HALF_COUNT = H // 2 * CG

    x_nat = x.rearrange("b h n c -> n b h c")
    out_pairs = out.rearrange("b h (j q) c -> b h j (q c)", q=2)

    with ExitStack() as ctx:
        def sb(name, shape, dt=f32):
            return ctx.enter_context(nc.sbuf_tensor(name, shape, dt))

        def pb(name):
            return ctx.enter_context(nc.psum_tensor(name, [P, 512], f32))

        def sem(name):
            return ctx.enter_context(nc.semaphore(name))

        x1_paired = sb("x1_paired", [P, H * W * J])
        rows = sb("rows", [P, 2, RG, W, J])
        x_sb = sb("x_sb", [P, 2, H * C])
        xs = sb("xs", [P, 2, CC])
        wh = sb("wh", [P, D, P], f32r)
        wl = sb("wl", [P, D, P], f32r)
        mix = sb("mix", [P, S, P])
        JP = J + 2 * EDGE
        carry_h = [sb(f"carry_h{s}", [P, WS, JP], f32r) for s in range(NS)]
        carry_l = [sb(f"carry_l{s}", [P, WS, JP], f32r) for s in range(NS)]
        carry = [sb(f"carry{s}", [P, SW]) for s in range(NS)]
        total = [sb(f"total{s}", [P, SW]) for s in range(NS)]
        staged = sb("staged", [P, 2, NS * SW])
        ident = sb("ident", [P, P])
        st1 = sb("st1", [P, 2, G, 3])
        dev = sb("dev", [P, 2, G])
        dev2 = sb("dev2", [P, 2, G])
        m2 = sb("m2", [P, 2, G])
        var1 = sb("var1", [P, G])
        std1 = sb("std1", [P, G])
        guess1 = sb("guess1", [P, G])
        square1 = sb("square1", [P, G])
        ratio1 = sb("ratio1", [P, G])
        rstd1 = sb("rstd1", [P, G])
        mean_rstd = sb("mean_rstd", [P, 2, G, CG])
        shift1 = sb("shift1", [P, 2])
        st2 = sb("st2", [P, 2 * CH, 6])
        mv = sb("mv", [P, 2])
        dev_c = sb("dev_c", [P, 1])
        var_p = sb("var_p", [P, 1])
        mean2_kept = sb("mean2_kept", [P, 1])
        var2 = sb("var2", [P, 1])
        rstd2 = sb("rstd2", [P, B])
        shift2 = sb("shift2", [P, B])
        bias_col = sb("bias_col", [P, 1])
        half_power = sb("half_power", [P, 1])
        inv256 = sb("inv256", [P, P])
        minus_avg = sb("minus_avg", [P, 1])
        group_avg = sb("group_avg", [P, 2, G, CG])
        w_raw = x1_paired[:, 0:D * P].rearrange("p (d m) -> p d m", d=D)
        at = D * P

        def scratch(n):
            nonlocal at
            at += n
            return x1_paired[:, at - n:at]
        dist = scratch(P)
        dist_i = scratch(P).bitcast(i32)
        dist2 = scratch(P)
        score = scratch(S * P).rearrange("p (s n) -> p s n", s=S)
        lin = scratch(S * P).rearrange("p (s n) -> p s n", s=S)
        prob = scratch(S * P).rearrange("p (s n) -> p s n", s=S)
        posmap = scratch(S * P).rearrange("p (s n) -> p s n", s=S)
        att_row = scratch(2 * S)
        proj_row = scratch(2 * S)
        proj = scratch(2 * S)
        neg_max = scratch(S)
        peak = scratch(S)
        exp_sum = scratch(S)
        inv_sum = scratch(S)
        ones_row = scratch(P)
        group_of = scratch(G)

        ps_conv = [pb(f"ps_conv{s}") for s in range(NS)]
        ps_mix = [pb(f"ps_mix{n}") for n in range(2)]
        ps_in = [pb(f"ps_in{n}") for n in range(2)]
        ps_out = pb("ps_out")
        ps_small = pb("ps_small")
        mean1 = ps_small[:, 0:G]
        var1_ps = ps_small[:, G:2 * G]
        shift1_ps = ps_small[:, 64:65]
        mean2 = ps_small[:, 66:67]
        var2_ps = ps_small[:, 68:69]

        w_loaded = sem("w_loaded")
        small_loaded = sem("small_loaded")
        bias_loaded = sem("bias_loaded")
        mix_ready = sem("mix_ready")
        w_zeroed = sem("w_zeroed")
        w_high = sem("w_high")
        setup_dve = sem("setup_dve")
        consts = sem("consts")
        pool_chain = sem("pool_chain")
        pool_consts = sem("pool_consts")
        proj_ps = sem("proj_ps")
        score_ready = sem("score_ready")
        prob_ready = sem("prob_ready")
        posmap_ready = sem("posmap_ready")
        posmap_t = sem("posmap_t")
        setup_done = sem("setup_done")
        x_loaded = [[sem(f"x_loaded{e}_{c}") for c in range(CH)] for e in range(2)]
        stats1_done = sem("stats1_done")
        mean1_ps = sem("mean1_ps")
        dev_ready = sem("dev_ready")
        dev2_ready = sem("dev2_ready")
        m2_ready = sem("m2_ready")
        var1_in_ps = sem("var1_in_ps")
        var1_ready = sem("var1_ready")
        std1_ready = sem("std1_ready")
        guess1_ready = sem("guess1_ready")
        square1_ready = sem("square1_ready")
        ratio1_ready = sem("ratio1_ready")
        rstd1_ready = sem("rstd1_ready")
        mean_rstd_ready = sem("mean_rstd_ready")
        shift1_in_ps = sem("shift1_in_ps")
        shift1_ready = sem("shift1_ready")
        xs_ready = sem("xs_ready")
        mix_done = [sem(f"mix_done{n}") for n in range(2)]
        x1_done = [sem(f"x1_done{n}") for n in range(2)]
        in_turned = sem("in_turned")
        in_kept = sem("in_kept")
        stats2_done = sem("stats2_done")
        mv_ready = sem("mv_ready")
        mean2_ps = sem("mean2_ps")
        dev_c_ready = sem("dev_c_ready")
        mean2_kept_ready = sem("mean2_kept_ready")
        var_p_ready = sem("var_p_ready")
        var2_in_ps = sem("var2_in_ps")
        var2_ready = sem("var2_ready")
        rstd2_ready = sem("rstd2_ready")
        shift2_ready = sem("shift2_ready")
        rows_ready = sem("rows_ready")
        conv_done = [sem(f"conv_done{s}") for s in range(NS)]
        carry_ready = [sem(f"carry_ready{s}") for s in range(NS)]
        high_ready = [sem(f"high_ready{s}") for s in range(NS)]
        low_ready = [sem(f"low_ready{s}") for s in range(NS)]
        total_ready = [sem(f"total_ready{s}") for s in range(NS)]
        out_turned = sem("out_turned")
        out_staged = sem("out_staged")
        stored = [sem(f"stored{n}") for n in range(2)]

        def x1_unit(wave, b, c, u):
            if wave == 1:
                v = x1_paired[:, bass.ds(b * (H * J) + (c * CR + u * HR) * J, HR * J)]
                return v.rearrange("p (h j) -> p h j", j=J)
            v = x1_paired[:, :].rearrange("p (h w j) -> p h w j", w=W, j=J)
            v = v[:, c * CR + u * HR:c * CR + (u + 1) * HR, bass.ds(b, 1), :]
            return v.rearrange("p h w j -> p h (w j)")

        def x1_rows(wave, it, row, n, b0, nb):
            if wave == 0:
                v = x1_paired[:, bass.ds(it * (STEPS * W * J) + row * W * J, n * W * J)]
                return v.rearrange("p (h w j) -> p h w j", h=n, w=W)[:, :, b0:b0 + nb, :]
            v = x1_paired[:, :].rearrange("p (w h j) -> p h w j", w=W, j=J)
            return v[:, bass.ds(it * STEPS + row, n), b0:b0 + nb, :]

        def alone(eng, done):
            eng.wait_ge(done, 1)

        def held(eng, n):
            return n if isinstance(n, int) else eng.to_reg(n)

        def is_zero(n):
            return isinstance(n, int) and n == 0

        def is_last(it):
            return isinstance(it, int) and it == ITERS - 1

        block = ctx.enter_context(nc.Block())

        @block.sync
        def _(sp):
            def load_chunk(b, e, c):
                if not (isinstance(b, int) and b < 2):
                    turned = held(sp, TU * b - 2 * TU + 2 * c + 2)
                    alone(sp, w_zeroed)
                    sp.wait_ge(in_turned, turned)
                sp.dma_start(x_sb[:, e, c * CC:(c + 1) * CC].rearrange("n (h c) -> n h c", c=C),
                             x_nat[:, bass.ds(b, 1), c * CR:(c + 1) * CR, :].rearrange("n b h c -> n (b h) c")
                             ).then_inc(x_loaded[e][c], 16)

            sp.dma_start(att_row[0:1, 0:S], centers.rearrange("s a -> a s")).then_inc(small_loaded, 16)
            sp.dma_start(att_row[0:1, S:2 * S], spreads.rearrange("s a -> a s")).then_inc(small_loaded, 16)
            for c in range(CH):
                load_chunk(0, 0, c)
            sp.dma_start(bias_col[:, :], token_bias.rearrange("a n e -> n (a e)")).then_inc(bias_loaded, 16)
            sp.wait_ge(w_zeroed, 1)
            for q in range(2):
                for o in range(2):
                    ds = [d for d in range(D) if 0 <= 2 * d + q - o < K]
                    k0 = 2 * ds[0] + q - o
                    sp.dma_start(w_raw[q * C:(q + 1) * C, ds[0]:ds[-1] + 1, o * C:(o + 1) * C],
                                 conv_w[k0:k0 + 2 * len(ds) - 1:2, :, :].rearrange("k c o -> c k o")
                                 ).then_inc(w_loaded, 16)
            for c in range(CH):
                load_chunk(1, 1, c)
            with sp.Fori(1, W // 2) as pair:
                for e in range(2):
                    for c in range(CH):
                        load_chunk(2 * pair + e, e, c)
            for n in range(CH + 2):
                load_chunk(W + n // CH, n // CH, n % CH)

            def store_row(wave, h, t, buf):
                staged_rows = held(sp, t)
                alone(sp, w_zeroed)
                sp.wait_ge(out_staged, staged_rows)
                src = staged[:, buf, :].rearrange("p (m f) -> p m f", f=P)
                for e in range(2):
                    dst = out_pairs[wave * W + e:(wave + 1) * W:2, bass.ds(h, 1), :, :]
                    sp.dma_start(dst.rearrange("m h j f -> (h j) m f"),
                                 src[e * J:(e + 1) * J, :, :]).then_inc(stored[buf], 16)

            def iteration(wave, it, b, e, more):
                for i in range(STEPS):
                    if not (is_zero(it) and i == 0):
                        store_row(wave, it * STEPS + i - 1, (it + wave * ITERS) * STEPS + i, (i + 1) % 2)
                    if i in (0, 2) and more >= 1:
                        load_chunk(b + 1, 1 - e, 2 + i // 2)
                    if i in (4, 6) and more >= 2:
                        load_chunk(b + 2, e, (i - 4) // 2)

            for e in range(2):
                iteration(0, e, W + e, e, 2)
            with sp.Fori(1, ITERS // 2 - 1) as pair:
                for e in range(2):
                    iteration(0, 2 * pair + e, 2 * pair + (W + e), e, 2)
            for e in range(2):
                iteration(0, ITERS - 2 + e, B - 2 + e, e, 1 - e)
            store_row(0, H - 1, H, 1)
            iteration(1, 0, None, None, 0)
            with sp.Fori(1, ITERS) as it:
                iteration(1, it, None, None, 0)
            store_row(1, H - 1, 2 * H, 1)
            for n in range(2):
                sp.wait_ge(stored[n], 2 * H // 2 * 32)

        @block.gpsimd
        def _(pool):
            nc.gpsimd.memset(ident[:, :], 0.0).then_inc(pool_chain, 1)
            nc.gpsimd.memset(group_of, 0.0).then_inc(pool_chain, 1)
            pool.wait_ge(pool_chain, 2)
            nc.gpsimd.affine_select(out=ident[:, :], in_=ident[:, :], compare_op=ALU.not_equal, fill=1.0,
                                    base=0, pattern=[[-1, P]], channel_multiplier=1).then_inc(pool_consts, 1)
            n = 2
            for q in range(2):
                for e in range(CG):
                    nc.gpsimd.affine_select(out=group_of, in_=group_of, compare_op=ALU.not_equal,
                                            fill=1.0 / (2 * CG), base=-(q * C + e), pattern=[[-CG, G]],
                                            channel_multiplier=1).then_inc(pool_chain, 1)
                    n += 1
                    pool.wait_ge(pool_chain, n)
            for q in range(2):
                for e in range(CG):
                    nc.gpsimd.tensor_copy(group_avg[:, q, :, e], group_of).then_inc(pool_consts, 1)
            nc.gpsimd.iota(dist_i, pattern=[[1, N]], base=0,
                           channel_multiplier=-1).then_inc(pool_consts, 1)

            def scale_chunk(b, e, c):
                n = b * CH + c
                if c == 0:
                    pool.wait_ge(rstd1_ready, b + 1)
                if not (isinstance(b, int) and n < 2):
                    for m in range(2):
                        pool.wait_ge(mix_done[m], n - 1)
                for m in range(2):
                    heads = slice(2 * m, 2 * m + 2)
                    src = x_sb[:, e, c * CC:(c + 1) * CC].rearrange("p (n s) -> p n s", s=S)[:, :, heads]
                    dst = xs[:, c % 2, :].rearrange("p (n s) -> p n s", s=S)[:, :, heads]
                    nc.gpsimd.tensor_tensor(dst.rearrange("p (h v) s -> p h v s", v=V),
                                            src.rearrange("p (h v) s -> p h v s", v=V),
                                            rstd1[:, m:G:2].unsqueeze(1).unsqueeze(3).to_broadcast([P, CR, V, CG]),
                                            ALU.mult).then_inc(xs_ready, 1)

            def rstd2_of(b):
                pool.wait_ge(var2_ready, b + 1)
                nc.gpsimd.tensor_tensor(rstd2[:, bass.ds(b, 1)], var2[:, :], half_power[:, 0:1],
                                        ALU.pow).then_inc(rstd2_ready, 1)

            def prep(b, e, i, prev, more):
                if i % 2 == 1 and i < STEPS - 1:
                    scale_chunk(b, e, (i + 1) // 2)
                if i == 6 and prev:
                    rstd2_of(b - 1)
                if i == 7 and more:
                    scale_chunk(b + 1, 1 - e, 0)

            def add_carry(wave, it, i, s):
                t = (it + wave * ITERS) * STEPS + i
                pool.wait_ge(carry_ready[s], t + 1)
                if not is_zero(t):
                    pool.wait_ge(out_turned, t)
                nc.gpsimd.tensor_tensor(total[s][:, :].rearrange("p (w j) -> p w j", w=WS),
                                        x1_rows(wave, it, i, 1, s * WS, WS)[:, 0, :, :],
                                        carry[s][:, :].rearrange("p (w j) -> p w j", w=WS),
                                        ALU.add).then_inc(total_ready[s], 1)

            def iteration(wave, it, b, e, prev, more):
                for i in range(STEPS):
                    for s in range(NS):
                        add_carry(wave, it, i, s)
                    if b is not None:
                        prep(b, e, i, prev, more)

            pool.wait_ge(consts, 1)
            scale_chunk(0, 0, 0)
            for e in range(2):
                for i in range(STEPS):
                    prep(e, e, i, e > 0, True)
            with pool.Fori(1, W // 2) as pair:
                for e in range(2):
                    for i in range(STEPS):
                        prep(2 * pair + e, e, i, True, True)
            rstd2_of(W - 1)
            for e in range(2):
                iteration(0, e, W + e, e, e > 0, True)
            with pool.Fori(1, ITERS // 2 - 1) as pair:
                for e in range(2):
                    iteration(0, 2 * pair + e, 2 * pair + (W + e), e, True, True)
            for e in range(2):
                iteration(0, ITERS - 2 + e, B - 2 + e, e, True, e == 0)
            rstd2_of(B - 1)
            with pool.Fori(0, ITERS) as it:
                iteration(1, it, None, None, False, False)

        @block.scalar
        def _(act):
            for s in range(S):
                act.wait_ge(score_ready, s + 1)
                nc.scalar.activation(prob[:, s, :], score[:, s, :], ACT.Exp, bias=neg_max[:, s:s + 1],
                                     accum_out=exp_sum[:, s:s + 1]).then_inc(prob_ready, 1)

            def std1_of(b):
                act.wait_ge(var1_ready, b + 1)
                nc.scalar.activation(std1[:, :], var1[:, :], ACT.Sqrt).then_inc(std1_ready, 1)

            def keep_in(b, e, wave, bw, c, u, free):
                n = b * CH + c
                act.wait_ge(shift1_ready, b + 1)
                half = held(act, 2 * n + u + 1)
                alone(act, setup_done)
                if free is not None:
                    for s in range(NS):
                        act.wait_ge(total_ready[s], free)
                act.wait_ge(in_turned, half)
                dst = x1_unit(wave, bw, c, u)
                for r in range(2):
                    src = ps_in[u][r * C:(r + 1) * C, :].rearrange("p (k j q) -> p q k j", k=HR // 2, q=2)
                    for q in range(2):
                        ins = nc.scalar.activation(dst[q * C:(q + 1) * C, r:HR:2, :], src[:, q, :, :],
                                                   ACT.Identity, bias=shift1[r * C:(r + 1) * C, e:e + 1])
                ins.then_inc(in_kept, 1)

            def mix_to_x1(b, e, c):
                act.wait_ge(mix_done[1], b * CH + c + 1)
                v = x_sb[:, e, c * CC:(c + 1) * CC].rearrange("p (n s) -> p s n", s=S)[:, 2:4, :]
                nc.scalar.activation(v, ps_mix[1][:, :].rearrange("p (s n) -> p s n", s=2), ACT.Identity,
                                     bias=bias_col[:, 0:1]).then_inc(x1_done[1], 1)

            def prep(b, e, wave, bw, i, prev, it):
                if it is None and i % 2 == 0 and i > 0:
                    mix_to_x1(b, e, i // 2 - 1)
                if it is None and i == 0 and prev:
                    mix_to_x1(b - 1, 1 - e, CH - 1)
                if i < 3 and prev:
                    c, u = (i + 5) // 2, (i + 5) % 2
                    keep_in(b - 1, 1 - e, wave, bw - 1, c, u, None if it is None else (it - 1) * STEPS + 2 * c + 2)
                if i >= 3:
                    c, u = (i - 3) // 2, (i - 3) % 2
                    keep_in(b, e, wave, bw, c, u, None if it is None else it * STEPS + 2 * c + 2)

            def finish(b, e, wave, bw, free):
                if wave == 0:
                    mix_to_x1(b, e, CH - 1)
                for n in range(5, TU):
                    keep_in(b, e, wave, bw, n // 2, n % 2, free)

            def norm_rows(wave, it, g, w):
                t = (it + wave * ITERS) * STEPS + g * RG
                if not (isinstance(t, int) and t < 2 * RG):
                    used = held(act, t - RG)
                    alone(act, setup_done)
                    for s in range(NS):
                        act.wait_ge(carry_ready[s], used)
                b = wave * W + w
                nc.scalar.activation(rows[:, g % 2, :, w, :], x1_rows(wave, it, g * RG, RG, w, 1)[:, :, 0, :],
                                     ACT.Identity, scale=rstd2[:, b:b + 1],
                                     bias=shift2[:, b:b + 1]).then_inc(rows_ready, 1)

            def stage_out(t, buf):
                act.wait_ge(out_turned, t)
                if not (isinstance(t, int) and t <= 2):
                    act.wait_ge(stored[buf], (t - 1 - buf) * 16)
                nc.scalar.activation(staged[:, buf, :], ps_out[:, :], ACT.Copy).then_inc(out_staged, 1)

            def iteration(wave, it, b, e, prev, more):
                first, last = is_zero(it), is_last(it)
                for i in range(STEPS):
                    t = (it + wave * ITERS) * STEPS + i
                    begins = first and i == 0
                    for s in range(NS):
                        if not (last and i == STEPS - 1):
                            act.wait_ge(carry_ready[s], t + 1)
                            nc.scalar.activation(carry_h[s][:, :, EDGE:EDGE + J],
                                                 carry[s][:, :].rearrange("p (w j) -> p w j", w=WS),
                                                 ACT.Copy).then_inc(high_ready[s], 1)
                        if s == 0 and not begins:
                            stage_out(t, (i + 1) % 2)
                        g = i // RG + 1
                        if not (last and g == GROUPS):
                            for k in range(2):
                                norm_rows(wave, it + g // GROUPS, g % GROUPS, (i % RG) * 2 * NS + 2 * s + k)
                        if s == 1 and i == 7 and more:
                            std1_of(b + 1)
                    if b is not None:
                        prep(b, e, 1, it, i, prev, it)

            def alone_prep(b, e, prev):
                for i in range(STEPS):
                    if i == 7:
                        std1_of(b + 1)
                    prep(b, e, 0, b, i, prev, None)

            std1_of(0)
            act.wait_ge(setup_done, 1)
            act.wait_ge(bias_loaded, 16)
            for e in range(2):
                alone_prep(e, e, e > 0)
            with act.Fori(1, W // 2) as pair:
                for e in range(2):
                    alone_prep(2 * pair + e, e, True)
            finish(W - 1, 1, 0, W - 1, None)
            for w in range(W):
                act.wait_ge(shift2_ready, w + 1)
                norm_rows(0, 0, 0, w)
            for e in range(2):
                iteration(0, e, W + e, e, e > 0, True)
            with act.Fori(1, ITERS // 2 - 1) as pair:
                for e in range(2):
                    iteration(0, 2 * pair + e, 2 * pair + (W + e), e, True, True)
            for e in range(2):
                iteration(0, ITERS - 2 + e, B - 2 + e, e, True, e == 0)
            finish(B - 1, 1, 1, W - 1, H)
            stage_out(H, 1)
            for w in range(W):
                act.wait_ge(shift2_ready, W + w + 1)
                norm_rows(1, 0, 0, w)
            iteration(1, 0, None, None, False, False)
            with act.Fori(1, ITERS - 1) as it:
                iteration(1, it, None, None, False, False)
            iteration(1, ITERS - 1, None, None, False, False)
            stage_out(2 * H, 1)

        @block.vector
        def _(dve):
            nc.vector.memset(w_raw, 0.0).then_inc(w_zeroed, 1)
            nc.vector.memset(half_power[:, :], -0.5).then_inc(consts, 1)
            nc.vector.memset(ones_row, 1.0)
            nc.vector.memset(inv256[:, :], 1.0 / (2 * P))
            nc.vector.memset(minus_avg[:, :], -1.0 / P)
            for s in range(NS):
                nc.vector.memset(carry_h[s][:, :, :].bitcast(f32), 0.0).then_inc(high_ready[s], 1)
                nc.vector.memset(carry_l[s][:, :, :].bitcast(f32), 0.0).then_inc(low_ready[s], 1)

            def stats1(b, e, half, first, count):
                for c in (2 * half, 2 * half + 1):
                    dve.wait_ge(x_loaded[e][c], 8 * (b - e) + 16)
                v = x_sb[:, e, 2 * half * CC:2 * (half + 1) * CC]
                v = v.rearrange("p (h m g e) -> p m h e g", m=G // 2, g=2, e=CG)
                for m in range(first, first + count):
                    ins = nc.vector.bn_stats(st1[:, half, 2 * m:2 * m + 2, :].rearrange("p g k -> p (g k)"),
                                             v[:, m, :, :, :])
                if half == 1 and first + count == G // 2:
                    ins.then_inc(stats1_done, 1)

            dve.wait_ge(small_loaded, 32)
            dve.wait_ge(pool_consts, 2 + 2 * CG)
            nc.vector.tensor_tensor(proj_row[0:1, 0:S], att_row[0:1, 0:S], att_row[0:1, S:2 * S], ALU.mult)
            nc.vector.tensor_scalar(proj_row[0:1, S:2 * S], att_row[0:1, S:2 * S], -0.5, None,
                                    ALU.mult).then_inc(setup_dve, 1)
            nc.vector.tensor_copy(dist, dist_i).then_inc(setup_dve, 1)
            dve.wait_ge(setup_dve, 2)
            nc.vector.tensor_tensor(dist2, dist, dist, ALU.mult).then_inc(setup_dve, 1)
            dve.wait_ge(proj_ps, 1)
            nc.vector.tensor_copy(proj, ps_small[:, 0:2 * S]).then_inc(setup_dve, 1)
            dve.wait_ge(setup_dve, 4)
            for s in range(S):
                nc.vector.tensor_scalar(lin[:, s, :], dist, proj[:, s:s + 1], None, ALU.mult).then_inc(setup_dve, 1)
            dve.wait_ge(setup_dve, 4 + S)
            for s in range(S):
                nc.vector.scalar_tensor_tensor(score[:, s, :], dist2, proj[:, S + s:S + s + 1], lin[:, s, :],
                                               ALU.mult, ALU.add).then_inc(setup_dve, 1)
            dve.wait_ge(setup_dve, 4 + 2 * S)
            nc.vector.reduce_max(peak, score, AX.X).then_inc(setup_dve, 1)
            dve.wait_ge(setup_dve, 5 + 2 * S)
            nc.vector.tensor_scalar(neg_max, peak, -1.0, None, ALU.mult).then_inc(score_ready, S)
            stats1(0, 0, 0, 0, G // 2)
            dve.wait_ge(prob_ready, S)
            nc.vector.reciprocal(inv_sum, exp_sum).then_inc(setup_dve, 1)
            dve.wait_ge(setup_dve, 6 + 2 * S)
            for s in range(S):
                nc.vector.tensor_scalar(posmap[:, s, :], prob[:, s, :], inv_sum[:, s:s + 1], None,
                                        ALU.mult).then_inc(posmap_ready, 1)
            stats1(0, 0, 1, 0, G // 2)
            dve.wait_ge(posmap_t, 1)
            turned = ps_in[0][:, :].rearrange("p (s m) -> p s m", s=S)
            nc.vector.tensor_copy(mix[:, :, :], turned).then_inc(mix_ready, 1)

            def spread(row):
                return row.unsqueeze(1).unsqueeze(3).to_broadcast([P, 2, G, CG])

            def deviations1(b):
                dve.wait_ge(mean1_ps, b + 1)
                nc.vector.tensor_tensor(dev[:, :, :], st1[:, :, :, 1],
                                        mean1.unsqueeze(1).to_broadcast([P, 2, G]),
                                        ALU.subtract).then_inc(dev_ready, 1)
                dve.wait_ge(dev_ready, b + 1)
                nc.vector.tensor_tensor(dev2[:, :, :], dev[:, :, :], dev[:, :, :], ALU.mult).then_inc(dev2_ready, 1)
                dve.wait_ge(dev2_ready, b + 1)
                nc.vector.scalar_tensor_tensor(m2[:, :, :], dev2[:, :, :], float(HALF_COUNT), st1[:, :, :, 2],
                                               ALU.mult, ALU.add).then_inc(m2_ready, 1)

            def variance1(b):
                dve.wait_ge(var1_in_ps, b + 1)
                nc.vector.tensor_scalar(var1[:, :], var1_ps, 1.0 / HALF_COUNT, EPS, ALU.mult,
                                        ALU.add).then_inc(var1_ready, 1)

            def rstd1_of(b):
                dve.wait_ge(std1_ready, b + 1)
                nc.vector.reciprocal(guess1[:, :], std1[:, :]).then_inc(guess1_ready, 1)
                dve.wait_ge(guess1_ready, b + 1)
                nc.vector.scalar_tensor_tensor(square1[:, :], guess1[:, :], -0.5, guess1[:, :],
                                               ALU.mult, ALU.mult).then_inc(square1_ready, 1)
                dve.wait_ge(square1_ready, b + 1)
                nc.vector.tensor_tensor(ratio1[:, :], square1[:, :], var1[:, :], ALU.mult).then_inc(ratio1_ready, 1)
                dve.wait_ge(ratio1_ready, b + 1)
                if not is_zero(b):
                    dve.wait_ge(xs_ready, 2 * CH * b)
                nc.vector.scalar_tensor_tensor(rstd1[:, :], ratio1[:, :], 1.5, guess1[:, :],
                                               ALU.add, ALU.mult).then_inc(rstd1_ready, 1)

            def mean_rstd1(b):
                dve.wait_ge(rstd1_ready, b + 1)
                nc.vector.tensor_tensor(mean_rstd[:, :, :, :], spread(mean1), spread(rstd1[:, :]),
                                        ALU.mult).then_inc(mean_rstd_ready, 1)

            def keep_shift1(b, e):
                dve.wait_ge(shift1_in_ps, b + 1)
                if not (isinstance(b, int) and b < 2):
                    dve.wait_ge(in_kept, TU * b - TU)
                nc.vector.tensor_copy(shift1[:, e:e + 1], shift1_ps).then_inc(shift1_ready, 1)

            def mix_to_x1(b, e, c, m):
                dve.wait_ge(mix_done[m], b * CH + c + 1)
                v = x_sb[:, e, c * CC:(c + 1) * CC].rearrange("p (n s) -> p s n", s=S)[:, 2 * m:2 * m + 2, :]
                nc.vector.scalar_tensor_tensor(v, ps_mix[m][:, :].rearrange("p (s n) -> p s n", s=2),
                                               bias_col[:, 0:1], v, ALU.add, ALU.add).then_inc(x1_done[m], 1)

            def stats2(b, wave, bw, c, u):
                if c == 0 and u == 0 and not is_zero(b):
                    dve.wait_ge(mv_ready, b)
                dve.wait_ge(in_kept, 2 * (b * CH + c) + u + 1)
                nc.vector.bn_stats(st2[:, 2 * c + u, :], x1_unit(wave, bw, c, u)).then_inc(stats2_done, 1)

            def moments2(b):
                seen = held(dve, TU * b + TU)
                alone(dve, consts)
                dve.wait_ge(stats2_done, seen)
                nc.vector.bn_aggr(mv[:, :], st2[:, :, :].rearrange("p n k -> p (n k)")).then_inc(mv_ready, 1)

            def deviations2(b):
                dve.wait_ge(mean2_ps, b + 1)
                nc.vector.tensor_tensor(dev_c[:, :], mv[:, 0:1], mean2, ALU.subtract).then_inc(dev_c_ready, 1)
                nc.vector.tensor_copy(mean2_kept[:, :], mean2).then_inc(mean2_kept_ready, 1)
                dve.wait_ge(dev_c_ready, b + 1)
                nc.vector.scalar_tensor_tensor(var_p[:, :], dev_c[:, :], dev_c[:, 0:1], mv[:, 1:2],
                                               ALU.mult, ALU.add).then_inc(var_p_ready, 1)

            def variance2(b):
                dve.wait_ge(var2_in_ps, b + 1)
                nc.vector.tensor_scalar(var2[:, :], var2_ps, EPS, None, ALU.add).then_inc(var2_ready, 1)

            def shift2_of(b):
                dve.wait_ge(rstd2_ready, b + 1)
                dve.wait_ge(mean2_kept_ready, b + 1)
                nc.vector.scalar_tensor_tensor(shift2[:, bass.ds(b, 1)], mean2_kept[:, :], -1.0, rstd2[:, bass.ds(b, 1)],
                                               ALU.mult, ALU.mult).then_inc(shift2_ready, 1)

            def prep(b, e, wave, bw, i, gap, prev, more):
                if gap == 0 and (i > 0 or prev) and (wave == 1 or i % 2 == 1):
                    if i > 0:
                        mix_to_x1(b, e, (i - 1) // 2, (i - 1) % 2)
                    else:
                        mix_to_x1(b - 1, 1 - e, 3, 1)
                if i == 7 and gap == 2 and prev:
                    shift2_of(b - 1)
                if i == 6 and gap == 3 and more:
                    deviations1(b + 1)
                if i == 7 and gap == 1 and more:
                    variance1(b + 1)
                if i == 7 and gap == 3 and more:
                    rstd1_of(b + 1)
                if i == 0 and gap == 2 and not is_zero(b):
                    mean_rstd1(b)
                if i == 2 and gap == 0 and not is_zero(b):
                    keep_shift1(b, e)
                if gap == 1:
                    if i >= 4:
                        stats2(b, wave, bw, (i - 4) // 2, (i - 4) % 2)
                    elif prev:
                        stats2(b - 1, wave, bw - 1, (i + 4) // 2, (i + 4) % 2)
                if i == 3 and gap == 3 and prev:
                    moments2(b - 1)
                if i == 4 and gap == 3 and prev:
                    deviations2(b - 1)
                if i == 5 and gap == 3 and prev:
                    variance2(b - 1)
                if more and i < 4:
                    stats1(b + 1, 1 - e, 0, 4 * i + gap, 1)
                if more and 4 <= i < 6:
                    stats1(b + 1, 1 - e, 1, 8 * (i - 4) + 2 * gap, 2)

            def finish(b, e, wave, bw):
                if wave == 1:
                    mix_to_x1(b, e, 3, 1)
                for n in range(4, TU):
                    stats2(b, wave, bw, n // 2, n % 2)
                moments2(b)
                deviations2(b)
                variance2(b)
                shift2_of(b)

            def iteration(wave, it, b, e, prev, more):
                last = is_last(it)
                for i in range(STEPS):
                    t = (it + wave * ITERS) * STEPS + i
                    for s in range(NS):
                        dve.wait_ge(conv_done[s], t + 1)
                        if i % RG == 0:
                            dve.wait_ge(rows_ready, W // RG * t + W)
                        if not is_zero(t):
                            dve.wait_ge(total_ready[s], t)
                        nc.vector.scalar_tensor_tensor(
                            carry[s][:, :], ps_conv[s][:, 0:SW], 0.0,
                            rows[:, (i // RG) % 2, i % RG, s * WS:(s + 1) * WS, :].rearrange("p w j -> p (w j)"),
                            ALU.max, ALU.add).then_inc(carry_ready[s], 1)
                        if b is not None:
                            prep(b, e, 1, it, i, 2 * s, prev, more)
                        if not (last and i == STEPS - 1):
                            dve.wait_ge(high_ready[s], t + 2)
                            nc.vector.tensor_tensor(carry_l[s][:, :, EDGE:EDGE + J],
                                                    carry[s][:, :].rearrange("p (w j) -> p w j", w=WS),
                                                    carry_h[s][:, :, EDGE:EDGE + J].bitcast(f32),
                                                    ALU.subtract).then_inc(low_ready[s], 1)
                        if b is not None:
                            prep(b, e, 1, it, i, 2 * s + 1, prev, more)

            def alone_prep(b, e, prev):
                for i in range(STEPS):
                    for gap in range(4):
                        prep(b, e, 0, b, i, gap, prev, True)

            deviations1(0)
            variance1(0)
            rstd1_of(0)
            dve.wait_ge(w_loaded, 64)
            nc.vector.tensor_copy(wh[:, :, :], w_raw).then_inc(w_high, 1)
            dve.wait_ge(w_high, 1)
            nc.vector.tensor_tensor(wl[:, :, :], w_raw, wh[:, :, :].bitcast(f32),
                                    ALU.subtract).then_inc(setup_done, 1)
            mean_rstd1(0)
            keep_shift1(0, 0)
            dve.wait_ge(bias_loaded, 16)
            for e in range(2):
                alone_prep(e, e, e > 0)
            with dve.Fori(1, W // 2) as pair:
                for e in range(2):
                    alone_prep(2 * pair + e, e, True)
            finish(W - 1, 1, 0, W - 1)
            for e in range(2):
                iteration(0, e, W + e, e, e > 0, True)
            with dve.Fori(1, ITERS // 2 - 1) as pair:
                for e in range(2):
                    iteration(0, 2 * pair + e, 2 * pair + (W + e), e, True, True)
            for e in range(2):
                iteration(0, ITERS - 2 + e, B - 2 + e, e, True, e == 0)
            for s in range(NS):
                nc.vector.memset(carry_h[s][:, :, :].bitcast(f32), 0.0).then_inc(high_ready[s], 1)
                nc.vector.memset(carry_l[s][:, :, :].bitcast(f32), 0.0).then_inc(low_ready[s], 1)
            finish(B - 1, 1, 1, W - 1)
            with dve.Fori(0, ITERS - 1) as it:
                iteration(1, it, None, None, False, False)
            iteration(1, ITERS - 1, None, None, False, False)

        @block.tensor
        def _(pe):
            pe.wait_ge(setup_dve, 1)
            nc.tensor.matmul(ps_small[:, 0:2 * S], ones_row[0:1, :], proj_row[0:1, :],
                             start=True, stop=True).then_inc(proj_ps, 1)
            pe.wait_ge(posmap_ready, S)
            pe.wait_ge(pool_consts, 1)
            for s in range(S):
                ins = nc.tensor.transpose(ps_in[0][:, s * P:(s + 1) * P], posmap[:, s, :], ident[:, :])
            ins.then_inc(posmap_t, 1)
            pe.wait_ge(mix_ready, 1)

            def average(ps, weights, srcs, done):
                for n, v in enumerate(srcs):
                    ins = nc.tensor.matmul(ps, weights, v, start=(n == 0), stop=(n == len(srcs) - 1))
                ins.then_inc(done, 1)

            def mix_bank(b, e, c, m, with_x=False):
                n = b * CH + c
                pe.wait_ge(xs_ready, 2 * n + m + 1)
                if not is_zero(n):
                    pe.wait_ge(x1_done[m], n)
                for s in (2 * m, 2 * m + 1):
                    head = ps_mix[m][:, (s % 2) * CR * V:(s % 2 + 1) * CR * V]
                    ins = nc.tensor.matmul(head, mix[:, s, :], xs[:, c % 2, s:CC:S], start=True, stop=not with_x)
                    if with_x:
                        ins = nc.tensor.matmul(head, ident[:, :], x_sb[:, e, c * CC + s:(c + 1) * CC:S],
                                               start=False, stop=True)
                ins.then_inc(mix_done[m], 1)

            def turn_in(b, e, c, u):
                n = b * CH + c
                for m in range(2):
                    pe.wait_ge(x1_done[m], n + 1)
                if not is_zero(n):
                    pe.wait_ge(in_kept, 2 * n - 1 + u)
                for k in range(HR // 2):
                    at = c * CC + (u * HR + 2 * k) * C
                    ins = nc.tensor.transpose(ps_in[u][:, k * P:(k + 1) * P], x_sb[:, e, at:at + P], ident[:, :])
                ins.then_inc(in_turned, 1)

            def mean1_of(b):
                pe.wait_ge(stats1_done, b + 1)
                average(mean1, inv256[:, :], [st1[:, half, :, 1] for half in range(2)], mean1_ps)

            def var1_of(b):
                pe.wait_ge(m2_ready, b + 1)
                average(var1_ps, inv256[:, :], [m2[:, half, :] for half in range(2)], var1_in_ps)

            def shift1_of(b):
                pe.wait_ge(mean_rstd_ready, b + 1)
                average(shift1_ps, mean_rstd[:, :, :, :].rearrange("p q g e -> p (q g e)"),
                        [minus_avg[:, :]], shift1_in_ps)

            def mean2_of(b):
                pe.wait_ge(mv_ready, b + 1)
                average(mean2, group_avg[:, :, :, :].rearrange("p q g e -> p (q g e)"), [mv[:, 0:1]], mean2_ps)

            def var2_of(b):
                pe.wait_ge(var_p_ready, b + 1)
                average(var2_ps, group_avg[:, :, :, :].rearrange("p q g e -> p (q g e)"), [var_p[:, :]], var2_in_ps)

            def prep(b, e, i, after, prev, more, scanning):
                if i == 1 and prev:
                    turn_in(b - 1, 1 - e, CH - 1, after)
                if i % 2 == 1 and i > 1:
                    turn_in(b, e, (i - 3) // 2, after)
                if after == 0:
                    if i == 7 and more:
                        var1_of(b + 1)
                else:
                    mix_bank(b, e, i // 2, i % 2, with_x=(i % 2 == 1 and not scanning))
                    if i == 1 and not is_zero(b):
                        shift1_of(b)
                    if i == 4 and prev:
                        mean2_of(b - 1)
                    if i == 5 and prev:
                        var2_of(b - 1)
                    if i == 6 and more:
                        if prev:
                            pe.wait_ge(var2_ready, b)
                        mean1_of(b + 1)

            def finish(b, e):
                for u in range(2):
                    turn_in(b, e, CH - 1, u)
                for s in range(NS):
                    convolve(0 if b < W else H, s)
                mean2_of(b)
                var2_of(b)

            def turn_out(t):
                if not (isinstance(t, int) and t <= 1):
                    pe.wait_ge(out_staged, t - 1)
                for s in range(NS):
                    pe.wait_ge(total_ready[s], t)
                    for m in range(WS // 2):
                        ins = nc.tensor.transpose(ps_out[:, s * SW + m * P:s * SW + (m + 1) * P],
                                                  total[s][:, m * P:(m + 1) * P], ident[:, :])
                ins.then_inc(out_turned, 1)

            def convolve(t, s):
                pe.wait_ge(high_ready[s], t + 1)
                for w in (wh, wl):
                    for d in range(D):
                        nc.tensor.matmul(ps_conv[s][:, 0:SW], w[:, d, :], carry_h[s][:, :, d:d + J],
                                         start=(w is wh and d == 0), stop=False)
                pe.wait_ge(low_ready[s], t + 1)
                for d in range(D):
                    ins = nc.tensor.matmul(ps_conv[s][:, 0:SW], wh[:, d, :], carry_l[s][:, :, d:d + J],
                                           start=False, stop=(d == D - 1))
                ins.then_inc(conv_done[s], 1)

            def iteration(wave, it, b, e, prev, more):
                for i in range(STEPS):
                    t = (it + wave * ITERS) * STEPS + i
                    for s in range(NS):
                        if not (i == 0 and is_zero(it)):
                            convolve(t, s)
                            if s == 0:
                                turn_out(t)
                        if b is not None:
                            prep(b, e, i, s, prev, more, True)

            def alone_prep(b, e, prev):
                for i in range(STEPS):
                    for after in range(2):
                        prep(b, e, i, after, prev, True, False)

            mean1_of(0)
            var1_of(0)
            shift1_of(0)
            for e in range(2):
                alone_prep(e, e, e > 0)
            with pe.Fori(1, W // 2) as pair:
                for e in range(2):
                    alone_prep(2 * pair + e, e, True)
            pe.wait_ge(setup_done, 1)
            finish(W - 1, 1)
            for e in range(2):
                iteration(0, e, W + e, e, e > 0, True)
            with pe.Fori(1, ITERS // 2 - 1) as pair:
                for e in range(2):
                    iteration(0, 2 * pair + e, 2 * pair + (W + e), e, True, True)
            for e in range(2):
                iteration(0, ITERS - 2 + e, B - 2 + e, e, True, e == 0)
            turn_out(H)
            finish(B - 1, 1)
            iteration(1, 0, None, None, False, False)
            with pe.Fori(1, ITERS) as it:
                iteration(1, it, None, None, False, False)
            turn_out(2 * H)


_INS = ['x', 'L0_conv_attention_centers', 'L0_conv_attention_spreads', 'L0_conv_token_proj_n_bias', 'L1_conv_W']
_OUTS = [((16, 64, 128, 64), 'float32')]


def kernel(**inputs):
    import numpy as _np
    import concourse.bacc as _bacc
    from concourse import mybir as _mybir
    from concourse.bass_utils import run_bass_kernel_spmd as _run

    nc = _bacc.Bacc("TRN2", target_bir_lowering=False, num_devices=1)
    arrays, args = {}, []
    for name in _INS:
        a = _np.ascontiguousarray(inputs[name])
        arrays[f"in_{name}_dram"] = a
        args.append(nc.dram_tensor(f"in_{name}_dram", a.shape, _mybir.dt.from_np(a.dtype), kind="ExternalInput").ap())
    for i, (shape, dtype) in enumerate(_OUTS):
        dt = _mybir.dt.from_np(_np.dtype(dtype))
        args.append(nc.dram_tensor(f"out_{i}_dram", shape, dt, kind="ExternalOutput").ap())
    mix_and_scan_kernel(nc, *args)
    r = _run(nc, [arrays], core_ids=[0])
    return r.results[0]["out_0_dram"]
```
